# Optimizing a Trainium2 kernel written in Bass

```python
import numpy as np
import jax
import jax.numpy as jnp

def _softmax(x, axis=-1):
    return jax.nn.softmax(x, axis=axis)

def _gelu(x):
    return jax.nn.gelu(x, approximate=True)

def _silu(x):
    return jax.nn.silu(x)

def _sigmoid(x):
    return jax.nn.sigmoid(x)

def _layernorm(x, axis=-1, eps=1e-05):
    m = jnp.mean(x, axis=axis, keepdims=True)
    v = jnp.var(x, axis=axis, keepdims=True)
    return (x - m) / jnp.sqrt(v + eps)

def _scatter_add(tgt, idx, src, axis=0):
    return tgt.at[idx].add(src)

def _segment_sum(src, seg, n):
    return jax.ops.segment_sum(src, seg, n)
kernel_name = 'mk_gps_d1_gnn_r8_8b9cd9'

def setup_inputs(seed: int=0):
    np.random.seed(seed)
    _w = jnp.asarray

    def _rec_inputs():
        import jax
        import jax.numpy as jnp
        _gk = jax.random.key(seed)
        x = -8.776e-05 + 1 * jax.random.normal(jax.random.fold_in(_gk, 1), (6250, 512), jnp.float32)
        src = jax.random.randint(jax.random.fold_in(_gk, 2), (100000,), 0, 6250, jnp.int32)
        dst = jax.random.randint(jax.random.fold_in(_gk, 3), (100000,), 0, 6250, jnp.int32)
        _o = jnp.argsort(dst, stable=True)
        src = src[_o]
        dst = dst[_o]
        return (x, src, dst)
    x, src, dst = _rec_inputs()

    def _L0_gnn_setup():
        import jax, jax.numpy as jnp
        import numpy as np
        N_NODES = 1250
        N_EDGES = 20000
        IN_DIM = 512
        OUT_DIM = 512
        LN_EPS = 1e-05
        key = jax.random.key(seed)
        k_x, k_src, k_ws, k_wn = jax.random.split(key, 4)
        x = jax.random.normal(k_x, (N_NODES, IN_DIM), dtype=jnp.float32)
        edge_src = jax.random.randint(k_src, (N_EDGES,), 0, N_NODES, dtype=jnp.int32)
        edge_dst = jnp.repeat(jnp.arange(N_NODES, dtype=jnp.int32), N_EDGES // N_NODES)
        deg = jnp.full((N_NODES,), float(N_EDGES // N_NODES), dtype=jnp.float32)
        scale = 1.0 / np.sqrt(IN_DIM)
        W_self = jax.random.normal(k_ws, (OUT_DIM, IN_DIM), dtype=jnp.float32) * scale
        W_neigh = jax.random.normal(k_wn, (OUT_DIM, IN_DIM), dtype=jnp.float32) * scale
        bias = jnp.zeros((OUT_DIM,), dtype=jnp.float32)
        gamma = jnp.ones((OUT_DIM,), dtype=jnp.float32)
        beta = jnp.zeros((OUT_DIM,), dtype=jnp.float32)
        return {'x': x, 'edge_src': edge_src, 'edge_dst': edge_dst, 'deg': deg, 'W_self': W_self, 'W_neigh': W_neigh, 'bias': bias, 'gamma': gamma, 'beta': beta}
    _L0_gnn_all = _L0_gnn_setup()
    _L0_gnn_in = {k: v for k, v in _L0_gnn_all.items() if k in ('W_self', 'W_neigh', 'bias', 'gamma', 'beta')}
    del _L0_gnn_all

    def _L0_mix_setup():
        import jax, jax.numpy as jnp
        import numpy as np
        HEADS = 8
        DIM_HEAD = 64
        DIM = 512
        INNER = HEADS * DIM_HEAD
        SCALE = DIM_HEAD ** (-0.5)

        def _feature_map(t):
            return jax.nn.elu(t) + 1.0
        key = jax.random.key(seed)
        k1, k2, k3, k4 = jax.random.split(key, 4)
        b, n = (8, 512)
        x = jax.random.normal(k1, (b, n, DIM), dtype=jnp.float32)
        w_qkv = jax.random.normal(k2, (INNER * 3, DIM), dtype=jnp.float32) * DIM ** (-0.5)
        w_out = jax.random.normal(k3, (DIM, INNER), dtype=jnp.float32) * INNER ** (-0.5)
        b_out = jax.random.normal(k4, (DIM,), dtype=jnp.float32) * 0.01
        return {'x': x, 'w_qkv': w_qkv, 'w_out': w_out, 'b_out': b_out}
    _L0_mix_all = _L0_mix_setup()
    _L0_mix_in = {k: v for k, v in _L0_mix_all.items() if k in ('w_qkv', 'w_out', 'b_out')}
    del _L0_mix_all

    def _L0_ffn_setup():
        import jax, jax.numpy as jnp
        import numpy as np
        B, S, D, F, E, NS, K = (2, 256, 512, 256, 8, 2, 2)
        key = jax.random.key(seed)
        ks = jax.random.split(key, 6)
        scale = 0.02

        def p(k, shape):
            return jax.random.normal(k, shape, jnp.float32) * scale
        return {'x': jax.random.normal(ks[0], (B, S, D), jnp.float32), 'gate_w': p(ks[1], (E, D)), 'gate_b': jnp.zeros((E,), jnp.float32), 'sw1': p(ks[2], (NS, F, D)), 'sb1': jnp.zeros((NS, F), jnp.float32), 'sw2': p(ks[3], (NS, D, F)), 'sb2': jnp.zeros((NS, D), jnp.float32), 'rw1': p(ks[4], (E, F, D)), 'rb1': jnp.zeros((E, F), jnp.float32), 'rw2': p(ks[5], (E, D, F)), 'rb2': jnp.zeros((E, D), jnp.float32)}
    _L0_ffn_all = _L0_ffn_setup()
    _L0_ffn_in = {k: v for k, v in _L0_ffn_all.items() if k in ('gate_w', 'gate_b', 'sw1', 'sb1', 'sw2', 'sb2', 'rw1', 'rb1', 'rw2', 'rb2')}
    del _L0_ffn_all
    return {'x': x, 'src': src, 'dst': dst, 'L0_gnn_W_self': _L0_gnn_in['W_self'], 'L0_gnn_W_neigh': _L0_gnn_in['W_neigh'], 'L0_gnn_bias': _L0_gnn_in['bias'], 'L0_gnn_gamma': _L0_gnn_in['gamma'], 'L0_gnn_beta': _L0_gnn_in['beta'], 'L0_mix_w_qkv': _L0_mix_in['w_qkv'], 'L0_mix_w_out': _L0_mix_in['w_out'], 'L0_mix_b_out': _L0_mix_in['b_out'], 'L0_ffn_gate_w': _L0_ffn_in['gate_w'], 'L0_ffn_gate_b': _L0_ffn_in['gate_b'], 'L0_ffn_sw1': _L0_ffn_in['sw1'], 'L0_ffn_sb1': _L0_ffn_in['sb1'], 'L0_ffn_sw2': _L0_ffn_in['sw2'], 'L0_ffn_sb2': _L0_ffn_in['sb2'], 'L0_ffn_rw1': _L0_ffn_in['rw1'], 'L0_ffn_rb1': _L0_ffn_in['rb1'], 'L0_ffn_rw2': _L0_ffn_in['rw2'], 'L0_ffn_rb2': _L0_ffn_in['rb2']}

def reference(x, src, dst, L0_gnn_W_self, L0_gnn_W_neigh, L0_gnn_bias, L0_gnn_gamma, L0_gnn_beta, L0_mix_w_qkv, L0_mix_w_out, L0_mix_b_out, L0_ffn_gate_w, L0_ffn_gate_b, L0_ffn_sw1, L0_ffn_sb1, L0_ffn_sw2, L0_ffn_sb2, L0_ffn_rw1, L0_ffn_rb1, L0_ffn_rw2, L0_ffn_rb2):
    import jax
    import jax.numpy as jnp

    def _L0_gnn_ref(x, edge_src, edge_dst, deg, W_self, W_neigh, bias, gamma, beta):
        import jax, jax.numpy as jnp
        import numpy as np
        N_NODES = 1250
        N_EDGES = 20000
        IN_DIM = 512
        OUT_DIM = 512
        LN_EPS = 1e-05
        n = x.shape[0]
        h_self = jnp.einsum('nd,od->no', x, W_self)
        neigh_sum = jax.ops.segment_sum(x[edge_src], edge_dst, num_segments=n)
        neigh_mean = neigh_sum / jnp.maximum(deg, 1.0)[:, None]
        h_neigh = jnp.einsum('nd,od->no', neigh_mean, W_neigh)
        h = h_self + h_neigh + bias
        mu = jnp.mean(h, axis=-1, keepdims=True)
        var = jnp.mean(jnp.square(h - mu), axis=-1, keepdims=True)
        h = (h - mu) * jax.lax.rsqrt(var + LN_EPS)
        return h * gamma + beta

    def _L0_mix_ref(x, w_qkv, w_out, b_out):
        import jax, jax.numpy as jnp
        import numpy as np
        HEADS = 8
        DIM_HEAD = 64
        DIM = 512
        INNER = HEADS * DIM_HEAD
        SCALE = DIM_HEAD ** (-0.5)

        def _feature_map(t):
            return jax.nn.elu(t) + 1.0
        b, n, _ = x.shape
        h, d = (HEADS, DIM_HEAD)
        qkv = x @ w_qkv.T
        q, k, v = jnp.split(qkv, 3, axis=-1)
        reshape = lambda t: t.reshape(b, n, h, d).transpose(0, 2, 1, 3)
        q, k, v = (reshape(q), reshape(k), reshape(v))
        q = _feature_map(q * SCALE)
        k = _feature_map(k)
        k_cumsum = k.sum(axis=2)
        context = jnp.einsum('bhnd,bhne->bhde', k, v)
        out = jnp.einsum('bhnd,bhde->bhne', q, context)
        denom = jnp.einsum('bhnd,bhd->bhn', q, k_cumsum)[..., None] + 1e-08
        out = out / denom
        out = out.transpose(0, 2, 1, 3).reshape(b, n, h * d)
        return out @ w_out.T + b_out

    def _L0_ffn_ref(x, gate_w, gate_b, sw1, sb1, sw2, sb2, rw1, rb1, rw2, rb2):
        import jax, jax.numpy as jnp
        import numpy as np
        B, S, D, F, E, NS, K = (2, 256, 512, 256, 8, 2, 2)
        b, s, d = x.shape
        t = x.reshape(-1, d)
        T = t.shape[0]
        hs = jax.nn.gelu(jnp.einsum('td,nfd->ntf', t, sw1) + sb1[:, None, :], approximate=False)
        shared = jnp.einsum('ntf,ndf->td', hs, sw2) + sb2.sum(axis=0)
        logits = t @ gate_w.T + gate_b
        probs = jax.nn.softmax(logits, axis=-1)
        top_v, top_i = jax.lax.top_k(probs, K)
        cw = jnp.zeros_like(probs).at[jnp.arange(T)[:, None], top_i].add(top_v)
        hr = jax.nn.gelu(jnp.einsum('td,efd->etf', t, rw1) + rb1[:, None, :], approximate=False)
        oe = jnp.einsum('etf,edf->etd', hr, rw2) + rb2[:, None, :]
        routed = jnp.einsum('etd,te->td', oe, cw)
        return (shared + routed).reshape(b, s, d)
    deg = jnp.maximum(jax.ops.segment_sum(jnp.ones(dst.shape, jnp.float32), dst, num_segments=6250), 1.0)
    xn = _layernorm(x, axis=-1)
    x = x + _L0_gnn_ref(xn, src, dst, deg, L0_gnn_W_self, L0_gnn_W_neigh, L0_gnn_bias, L0_gnn_gamma, L0_gnn_beta) + _L0_mix_ref(xn[None], L0_mix_w_qkv, L0_mix_w_out, L0_mix_b_out)[0]
    x = x + _L0_ffn_ref(_layernorm(x, axis=-1)[None], L0_ffn_gate_w, L0_ffn_gate_b, L0_ffn_sw1, L0_ffn_sb1, L0_ffn_sw2, L0_ffn_sb2, L0_ffn_rw1, L0_ffn_rb1, L0_ffn_rw2, L0_ffn_rb2)[0]
    return x

_drawn_inputs = setup_inputs


def setup_inputs(seed=0):
    import zlib

    import numpy as np

    out = dict(_drawn_inputs(seed))
    spreads = {'L0_gnn_bias': (0.0, 0.1),
     'L0_gnn_gamma': (1.0, 0.2),
     'L0_gnn_beta': (0.0, 0.1),
     'L0_ffn_gate_b': (0.0, 0.69),
     'L0_ffn_sb1': (0.0, 0.421),
     'L0_ffn_sb2': (0.0, 0.1),
     'L0_ffn_rb1': (0.0, 0.8),
     'L0_ffn_rb2': (0.0, 0.406)}
    factors = {'L0_mix_w_qkv': 5.307,
     'L0_mix_w_out': 5.085,
     'L0_mix_b_out': 8.0,
     'L0_ffn_rw1': 3.57,
     'L0_ffn_rw2': 3.342}
    for name, (base, spread) in spreads.items():
        noise = np.random.default_rng([zlib.crc32(name.encode()), seed]).standard_normal(out[name].shape)
        drawn = base * np.exp(spread * noise) if base else spread * noise
        out[name] = jnp.asarray(drawn.astype(out[name].dtype))
    for name, factor in factors.items():
        out[name] = (out[name] * factor).astype(out[name].dtype)
    return out
```

```python
from contextlib import ExitStack

import concourse.bass as bass
from concourse import mybir

ALU = mybir.AluOpType
ACT = mybir.ActivationFunctionType
AX_X = mybir.AxisListType.X
F32 = mybir.dt.float32
F16 = mybir.dt.float16
I32 = mybir.dt.int32
U32 = mybir.dt.uint32
RMAX = bass.bass_isa.ReduceOp.max

N, D = 6250, 512
E_EDGES = 100000
T = 125
NT = N // T
G = 2
NG = NT // G
GT = G * T
KC = D // 128
SLOTS = 17
SPAN = SLOTS * 128
EPAD = E_EDGES + SPAN
EP, EC = 125, E_EDGES // 125
NE, FE = 8, 256
NS = 2
FC = (NS + NE) * FE // 128
CH = 256
CAP = -(-N // CH) * CH
MINS = -(-2 * N // CH)
MAXS = 2 * N // CH + 2 * NE
SPLIT = 9
NEWTON = 3
HID = (NS + NE) * FE
EPS = 1e-5

XS = 2048.0
QS = 16384.0
KVQ, SN, W1, W2, GW, HB, MH = range(7)
PER2 = FC // KC


def gps_layer_kernel(nc, x, edges, dst_flat, w_kv, w_q, w_sn, w_out, w_gate, w_1, w_2, b_1, b_2, rows, gate_b, out):
    table = nc.dram_tensor("table", [N, 2 * D], F16).ap()
    xnt = nc.dram_tensor("xnt", [NG, 128, 2 * KC * GT], F16).ap()
    x2d = nc.dram_tensor("x2d", [N, D], F32).ap()
    table2 = nc.dram_tensor("table2", [N, 2 * D], F16).ap()
    x2t = nc.dram_tensor("x2t", [NG, 128, 2 * KC * GT], F16).ap()
    slots = nc.dram_tensor("slots", [NE * CAP, 1], I32).ap()
    yd = nc.dram_tensor("yd", [MAXS * CH, D], F32).ap()

    with ExitStack() as ctx:
        def sb(name, shape, dt):
            return ctx.enter_context(nc.sbuf_tensor(name, shape, dt))

        names = """
            dst_in kvq_in sn_in w1_in w2_in small_in rows_in wout_in
            consts iota_set ident_set
            mx_done mx_all mx_scale w_conv_hi w_conv_lo
            edge_cast edge_viol edge_cnt edge_sum edge_step sched_set
            x_in0 x_in1 ln_step ln_var ln_rs ln_out
            xn_hi xn_lo tab_out0 tab_out1 xt_ps xt_hi xt_lo xt_out
            k_ps k_neg v_ps k_exp k_relu v_sb kf ksum_add ctx_ps
            ksum_ps m_ps ctx_sb ksum_sb kinv_set beta_set mf_set mf_max mh_all mh_scale mh_hi mh_done
            xt_in xg_in q_ps q_neg q_exp q_relu q_phi q_u den_ps q_den q_rec q_hat q_hi q_lo
            e_in gathered_a gathered_b onehot onehot_cnt deg_step ring_in agg_half agg_ps agg_end mean_sb
            mt_ps mt_hi mt_lo h_ps h_sb h_step h_gam h_res xb att_ps x2_sb z_step
            tn_sb tn_hi tn_lo tt_ps tt_sb gate_ps gate_dve gate_exp pos_ps
            rows2_out x2t_out x2_out scat slots_out disp_set yd_pos cnt_ps cnt_step sched2_set
            b2_in ix_in g_in ct_ps ct_act ct_dve ch_ps c_gelu c_hi c_lo cp_ps y_sb y_st
            sb2_in sb2_sum dt_in0 dt_in1 dx_in yi_set yg_in d_f1 d_gelu d_hi d_lo d_f2 d_y d_res d_out
        """.split()
        sem = {n: ctx.enter_context(nc.semaphore(n)) for n in names}

        def pair(name):
            return [sem[name + "0"], sem[name + "1"]]

        Wsn = sb("Wsn", [128, 2, 8, D], F16)
        Wq = sb("Wq", [128, 2, KC, D], F16)
        Mh = sb("Mh", [128, 2, KC, D], F16)
        Wff = sb("Wff", [128, 2 * KC, 2, HID], F16)
        Wg = sb("Wg", [128, 2, KC, NE], F16)
        wgf = sb("wgf", [128, KC * NE], F32)
        b1 = sb("b1", [128, FC], F32)
        bias_bc = sb("bias_bc", [128, D], F32)
        gamma_bc = sb("gamma_bc", [128, D], F32)
        beta_bc = sb("beta_bc", [128, D], F32)
        gateb_bc = sb("gateb_bc", [128, NE], F32)
        ident = sb("ident", [128, 128], F32)
        blk = sb("blk", [128, 128], F32)
        ones = sb("ones", [128, 1], F32)
        ones16 = sb("ones16", [128, 1], F16)
        half = sb("half", [128, 1], F32)
        tiny = sb("tiny", [128, 1], F32)
        zeros16 = sb("zeros16", [1, D], F16)
        iota_i = sb("iota_i", [128, T], I32)
        iota_f = sb("iota_f", [128, T], F32)
        iota_e = sb("iota_e", [128, NE], F32)
        ebuf = [sb(f"ebuf{j}", [128, 2 * SLOTS], I32) for j in range(G)]
        ohs = sb("ohs", [128, SLOTS * T + SLOTS * T % 2], F16)
        oh = ohs[:, 0:SLOTS * T].rearrange("p (s n) -> p s n", s=SLOTS)
        ohc = sb("ohc", [128, T], F16)
        no_nodes = ohs[:, 0:2 * NE * CAP // 128].bitcast(I32)
        after = ohs[0:T, 0:2 * 3 * 2 * NT].bitcast(F32).rearrange("p (r n) -> p r n", r=3)
        row2 = ohs[0:T, 2 * 6 * NT:2 * 6 * NT + 2 * 64].bitcast(F32).rearrange("p (r n) -> p r n", r=4)
        mx = sb("mx", [128, 24], F32)
        mg = sb("mg", [128, 8], F32)
        ma = sb("ma", [128, 8], F32)
        mp = sb("mp", [128, 8], F32)
        sg = sb("sg", [128, 8], F32)
        si = sb("si", [128, 8], F32)
        sv = sb("sv", [128, 8], F32)
        S_KV, S_Q, S_H, S_W1, S_W2, S_G, S_ATT = range(7)
        ksum = sb("ksum", [128, KC], F32)
        kinv = sb("kinv", [128, KC], F32)
        sched = sb("sched", [1, 2, 64], I32)
        st = sb("st", [T, 2, 6], F32)
        mv = sb("mv", [T, 2, 2], F32)
        vs = sb("vs", [T, 2, 1], F32)
        rs = sb("rs", [T, 2, 1], F32)
        dg = sb("dg", [T, 2, 2], F32)
        y0 = sb("y0", [T, 2], F32)
        gl = sb("gl", [T, 2, NE], F32)
        g8 = sb("g8", [T, 2, 8], F32)
        gi = sb("gi", [T, 2, 8], U32)
        gif = sb("gif", [T, 2, 2], F32)
        gs = sb("gs", [T, 2, 4], F32)
        ge = sb("ge", [T, 2, NE], F32)
        ew = sb("ew", [T, 2, 2], F32)
        choice = sb("choice", [T, 2, 2, NE], F32)
        chosen = sb("chosen", [T, 2, NE], F16)
        before = sb("before", [T, NE], F16)
        place = sb("place", [T, 2, NE], F32)
        placed = sb("placed", [T, 2, 2, NE], F32)
        posf = sb("posf", [T, 2, 2], F32)
        posi = sb("posi", [T, 2, 2], I32)
        tok = sb("tok", [T, 2], I32)
        eoff = sb("eoff", [128, NE], F32)
        wk = sb("wk", [T, NT, 2], F32)
        pos = sb("pos", [T, NT, 2], I32)
        yi = sb("yi", [T, 4], I32)
        wcur = sb("wcur", [T, 4], F32)
        tri16 = sb("tri16", [128, 128], F16)
        ident16 = sb("ident16", [128, 128], F16)
        ones16w = sb("ones16w", [128, 128], F16)
        idx = sb("idx", [128, 2], I32)
        sched2 = sb("sched2", [T, 16], I32)

        RING = SLOTS * 2 * D // 2
        region1 = sb("region1", [128, RING], F32)
        ring = region1[:, :].bitcast(F16).rearrange("p (s n) -> p s n", s=SLOTS)
        at = [0]

        def carve(region, n, dt=F32, parts=128):
            words = n if dt == F32 else n // 2
            v = region[0:parts, at[0]:at[0] + words]
            at[0] += words
            assert at[0] <= region.shape[1]
            return v if dt == F32 else v.bitcast(dt)

        xa = [carve(region1, D, parts=T) for _ in range(2)]
        xn = [carve(region1, D, parts=T) for _ in range(2)]
        tab = [carve(region1, 2 * D, F16, T) for _ in range(2)]
        xT = carve(region1, 2 * KC * GT, F16).rearrange("p (s k n) -> p s k n", s=2, k=KC)
        ke = [carve(region1, D, parts=T) for _ in range(2)]
        kr = [carve(region1, D, parts=T) for _ in range(2)]
        kf = [carve(region1, D, parts=T) for _ in range(2)]
        vf = [carve(region1, D, parts=T) for _ in range(2)]
        kacc = carve(region1, D, parts=T)
        at[0] = 0
        tg = carve(region1, 2 * 2 * D, F16).rearrange("p (c n) -> p c n", c=2)
        tTc = carve(region1, 2 * KC * CH, F16).rearrange("p (s k n) -> p s k n", s=2, k=KC)
        gelc = carve(region1, 2 * CH).rearrange("p (c n) -> p c n", c=2)
        hTc = carve(region1, 2 * 2 * CH, F16).rearrange("p (s c n) -> p s c n", s=2, c=2)
        ysb = carve(region1, 2 * D).rearrange("p (c n) -> p c n", c=2)
        b2bc = carve(region1, NE * D).rearrange("p (e n) -> p e n", e=NE)

        region2 = sb("region2", [128, 11168], F32)
        at[0] = 0
        Wkv = carve(region2, 2 * KC * 2 * D, F16).rearrange("p (s k n) -> p s k n", s=2, k=KC)
        WoutT = carve(region2, KC * D).rearrange("p (k n) -> p k n", k=KC)
        ctxT = carve(region2, KC * 128).rearrange("p (k n) -> p k n", k=KC)
        Mf = carve(region2, KC * D).rearrange("p (k n) -> p k n", k=KC)
        cnt = carve(region2, 64)
        thr = carve(region2, 64)
        row = carve(region2, 8 * 64, parts=1).rearrange("p (r n) -> p r n", r=8)
        tri = carve(region2, 128)
        d_f = carve(region2, EC)
        junk = carve(region2, EC)
        at[0] = 0
        d_i = carve(region2, EC).bitcast(I32)
        n_i = carve(region2, EC).bitcast(I32)
        at[0] = 0
        xg = carve(region2, G * D, parts=T).rearrange("p (j n) -> p j n", j=G)
        xTg = carve(region2, 2 * KC * GT, F16).rearrange("p (s k n) -> p s k n", s=2, k=KC)
        qe = carve(region2, KC * GT).rearrange("p (k n) -> p k n", k=KC)
        hh = carve(region2, G * D)
        qr = hh[:, 0:KC * GT].rearrange("p (k n) -> p k n", k=KC)
        hh = hh[0:T, :].rearrange("p (j n) -> p j n", j=G)
        qh = carve(region2, 2 * KC * GT, F16).rearrange("p (s k n) -> p s k n", s=2, k=KC)
        mean = carve(region2, G * D, parts=T).rearrange("p (j n) -> p j n", j=G)
        tn = carve(region2, G * D, parts=T).rearrange("p (j n) -> p j n", j=G)
        tab2 = carve(region2, 2 * G * D, F16, T).rearrange("p (j n) -> p j n", j=G)
        tT = carve(region2, 2 * KC * GT, F16).rearrange("p (s k n) -> p s k n", s=2, k=KC)
        x2 = carve(region2, G * D, parts=T).rearrange("p (j n) -> p j n", j=G)
        mT = carve(region2, 2 * KC * GT, F16).rearrange("p (s k n) -> p s k n", s=2, k=KC)
        at[0] = 0
        tTd = [carve(region2, 2 * KC * GT, F16).rearrange("p (s k n) -> p s k n", s=2, k=KC) for _ in range(2)]
        geld = [carve(region2, 2 * GT).rearrange("p (c n) -> p c n", c=2) for _ in range(NS)]
        hTd = [carve(region2, 2 * 2 * GT, F16).rearrange("p (s c n) -> p s c n", s=2, c=2) for _ in range(NS)]
        acc = carve(region2, G * D, parts=T).rearrange("p (j n) -> p j n", j=G)
        yr = carve(region2, G * 2 * D, parts=T).rearrange("p (j k n) -> p j k n", j=G, k=2)
        res = carve(region2, G * D, parts=T).rearrange("p (j n) -> p j n", j=G)
        sb2 = carve(region2, 2 * D, parts=T).rearrange("p (j n) -> p j n", j=2)

        bank = [ctx.enter_context(nc.psum_tensor(f"bank{b}", [128, 512], F32)) for b in range(8)]

        def two(b):
            return bank[b][:, 0:2 * GT].rearrange("p (c n) -> p c n", c=2)

        def four(b):
            return bank[b][:, 0:KC * T].rearrange("p (c n) -> p c n", c=KC)

        def parts16(b, n):
            return bank[b][:, :].bitcast(F16).rearrange("p (s k n) -> p s k n", s=2, k=KC)[:, :, :, 0:n]

        def both(j):
            return slice(j * T, (j + 1) * T)

        def w1(part, k, f):
            return Wff[:, k, part, f]

        def w2(part, f):
            return Wff[:, KC + f // PER2, part, f % PER2 * D:(f % PER2 + 1) * D]

        assert PER2 * D == HID
        pieces1 = [w_1[:, k * HID:(k + 1) * HID] for k in range(KC)]
        pieces2 = [w_2[:, k * HID:(k + 1) * HID] for k in range(KC)]
        waiting = [Wff[:, k].rearrange("p s n -> p (s n)").bitcast(F32) for k in range(1, 2 * KC)]
        waiting.append(region1[:, 3 * 2048:3 * 2048 + HID])
        wlist = [(w_kv, region1[:, 0:2 * 2048], Wkv.rearrange("p s k n -> p s (k n)"), KVQ, "kvq_in"),
                 (w_q, region1[:, 2 * 2048:3 * 2048], Wq[:].rearrange("p s k n -> p s (k n)"), KVQ, "kvq_in"),
                 (w_sn, region2[:, 4096:8192], Wsn[:].rearrange("p s k n -> p s (k n)"), SN, "sn_in")]
        wlist += [(p, waiting[k], Wff[:, k], W1 if k < KC else W2, "w1_in" if k < KC else "w2_in")
                  for k, p in enumerate(pieces1 + pieces2)]
        NW = len(wlist)
        FF = NW - 2 * KC
        order = [FF, 0, FF + 1, 1, FF + 2, 2] + list(range(FF + 3, NW))
        wmm = nc.tensor.matmul

        def three(ps, xh, xl, wh, wl, first, last):
            wmm(ps, xh, wh, start=first, stop=False)
            wmm(ps, xh, wl, start=False, stop=False)
            return wmm(ps, xl, wh, start=False, stop=last)

        def past(i):
            return not isinstance(i, int) or i > 0

        def of(eng, value):
            return value if isinstance(value, int) else eng.to_reg(value)

        block = ctx.enter_context(nc.Block())

        @block.sync
        def _(sp):
            sp.dma_start(d_i[0:EP, :], dst_flat[0:E_EDGES].rearrange("(p c) -> p c", p=EP)).then_inc(sem["dst_in"], 16)
            sp.dma_start(n_i[0:EP, :], dst_flat[1:E_EDGES + 1].rearrange("(p c) -> p c", p=EP)).then_inc(sem["dst_in"], 16)
            sp.dma_start(wgf[:], w_gate).then_inc(sem["small_in"], 16)
            sp.dma_start(b1[:], b_1).then_inc(sem["small_in"], 16)
            sp.dma_start(gateb_bc[:], gate_b.partition_broadcast(128)).then_inc(sem["small_in"], 16)
            for r, t in enumerate((bias_bc, gamma_bc, beta_bc)):
                sp.dma_start(t[:], rows[r:r + 1, :].partition_broadcast(128)).then_inc(sem["rows_in"], 16)
            for src, held, _, _, loaded in wlist:
                sp.dma_start(held, src).then_inc(sem[loaded], 16)
            sp.wait_ge(sem["edge_viol"], 2)
            sp.wait_ge(sem["w_conv_hi"], NW + 1)
            sp.wait_ge(sem["w_conv_lo"], NW + 1)
            sp.dma_start(WoutT, w_out.rearrange("p (k n) -> p k n", k=KC)).then_inc(sem["wout_in"], 16)
            sp.dma_start(Mf[0:T, 0, :], rows[3:4, :].partition_broadcast(T)).then_inc(sem["wout_in"], 16)

            def nodes(i):
                for j in range(G):
                    if past(i):
                        sp.wait_ge(sem["ln_out"], 2 * i + j - 1)
                    sp.dma_start(xa[j], x[bass.ds(i * GT + j * T, T), :]).then_inc(pair("x_in")[j], 16)

            nodes(0)
            with sp.Fori(1, NG) as i:
                nodes(i)

            def edge_steps(g, j):
                t = 2 * g + j
                first = sp.value_load(sched[0:1, 0, bass.ds(t, 1)], min_val=0, max_val=E_EDGES)
                lo = sp.value_load(sched[0:1, 1, bass.ds(t, 1)], min_val=0, max_val=4000)
                hi = sp.value_load(sched[0:1, 1, bass.ds(t + 1, 1)], min_val=1, max_val=4000)
                with sp.Fori(lo, hi) as r:
                    later = (r - lo + 63) // 64 & 1
                    halves, rows = sp.to_reg(r + 1), sp.to_reg(later * r + 1)
                    sp.wait_ge(sem["agg_half"], halves)
                    sp.wait_ge(sem["ring_in"], rows)
                    off = nc.s_assert_within((first + (r - lo) * SPAN) * 2, 0, 2 * E_EDGES,
                                              skip_runtime_bounds_check_because="a tile has edges / SPAN steps, rounded up")
                    sp.dma_start(ebuf[j][:], edges[bass.ds(off, 2 * SPAN)].rearrange("(p q) -> p q", p=128)).then_inc(sem["e_in"], 16)

            sp.wait_ge(sem["sched_set"], 1)
            edge_steps(0, 0)
            for j in range(G):
                sp.wait_ge(pair("tab_out")[j], 16 * NG)
            sp.wait_ge(sem["xt_out"], 16 * NG)
            sp.wait_ge(sem["m_ps"], KC)

            def load_xt(i):
                if past(i):
                    sp.wait_ge(sem["h_ps"], 2 * i)
                sp.dma_start(xTg.rearrange("p s k n -> p (s k n)"), xnt[bass.ds(i, 1), :, :].rearrange("a p n -> (a p) n")).then_inc(sem["xt_in"], 16)

            def load_x(i):
                if past(i):
                    sp.wait_ge(sem["h_res"], 2 * i)
                sp.dma_start(xg, x[bass.ds(i * GT, GT), :].rearrange("(j p) n -> p j n", j=G)).then_inc(sem["xg_in"], 16)

            def store_x2(i):
                sp.wait_ge(sem["x2_sb"], 2 * i + 2)
                sp.dma_start(x2d[bass.ds(i * GT, GT), :].rearrange("(j p) n -> p j n", j=G), x2).then_inc(sem["x2_out"], 16)

            def store_normalised(i):
                sp.wait_ge(sem["tn_hi"], 2 * i + 2)
                sp.wait_ge(sem["tn_lo"], 2 * i + 2)
                sp.dma_start(table2[bass.ds(i * GT, GT), :].rearrange("(j p) n -> p j n", j=G), tab2).then_inc(sem["rows2_out"], 16)
                sp.wait_ge(sem["tt_sb"], 2 * i + 2)
                sp.dma_start(x2t[bass.ds(i, 1), :, :].rearrange("a p n -> (a p) n"), tT.rearrange("p s k n -> p (s k n)")).then_inc(sem["x2t_out"], 16)

            def group(i, prev, nxt):
                if nxt is not None:
                    edge_steps(nxt, 0)
                if nxt is not None:
                    edge_steps(nxt, 1)
                if prev is not None:
                    store_normalised(prev)
                if nxt is not None:
                    load_xt(nxt)
                    load_x(nxt)
                store_x2(i)

            edge_steps(0, 1)
            load_xt(0)
            load_x(0)
            group(0, None, 1)
            with sp.Fori(1, NG - 1) as i:
                group(i, i - 1, i + 1)
            group(NG - 1, NG - 2, None)
            store_normalised(NG - 1)

            sp.wait_ge(sem["agg_end"], NT)
            for e in range(NE):
                sp.dma_start(b2bc[:, e, :], b_2[e:e + 1, :].partition_broadcast(128)).then_inc(sem["b2_in"], 16)
            sp.wait_ge(sem["sched2_set"], 1)
            sp.wait_ge(sem["scat"], 64 * NG)
            for e in range(NE):
                lo = sp.value_load(sched2[0:1, e:e + 1], min_val=2 * e, max_val=400) if e else 0
                hi = sp.value_load(sched2[0:1, e + 1:e + 2], min_val=2 * e + 2, max_val=400)
                if e == 0:
                    sp.dma_start(idx[:], slots[0:CH, :].rearrange("(p c) o -> p (c o)", p=128)).then_inc(sem["ix_in"], 16)
                with sp.Fori(lo if e else 1, hi) as r:
                    sp.wait_ge(sem["g_in"], r * 32)
                    off = nc.s_assert_within((r - lo) * CH + e * CAP, e * CAP, (e + 1) * CAP - CH,
                                              skip_runtime_bounds_check_because="an expert has tokens / CH steps, rounded up")
                    sp.dma_start(idx[:], slots[bass.ds(off, CH), :].rearrange("(p c) o -> p (c o)", p=128)).then_inc(sem["ix_in"], 16)

            sp.wait_ge(sem["x2_out"], 16 * NG)
            sp.wait_ge(sem["rows2_out"], 16 * NG)
            sp.wait_ge(sem["x2t_out"], 16 * NG)
            for k in range(NS):
                sp.dma_start(sb2[:, k, :], b_2[NE + k:NE + k + 1, :].partition_broadcast(T)).then_inc(sem["sb2_in"], 16)

            def load_turned(i, b, used=True):
                if used:
                    sp.wait_ge(sem["d_f1"], 2 * i - 2)
                sp.dma_start(tTd[b].rearrange("p s k n -> p (s k n)"), x2t[bass.ds(i, 1), :, :].rearrange("a p n -> (a p) n")).then_inc(pair("dt_in")[b], 16)

            def loads(i):
                if past(i):
                    sp.wait_ge(sem["d_res"], 2 * i)
                sp.dma_start(acc, x2d[bass.ds(i * GT, GT), :].rearrange("(j p) n -> p j n", j=G)).then_inc(sem["dx_in"], 16)

            def store(i):
                sp.wait_ge(sem["d_res"], 2 * i + 2)
                sp.dma_start(out[bass.ds(i * GT, GT), :].rearrange("(j p) n -> p j n", j=G), res).then_inc(sem["d_out"], 16)

            load_turned(0, 0, False)
            loads(0)
            load_turned(1, 1, False)
            with sp.Fori(0, (NG - 3) // 2) as m:
                load_turned(2 * m + 2, 0)
                loads(2 * m + 1)
                store(2 * m)
                load_turned(2 * m + 3, 1)
                loads(2 * m + 2)
                store(2 * m + 1)
            load_turned(NG - 1, 0)
            loads(NG - 2)
            store(NG - 3)
            loads(NG - 1)
            store(NG - 2)
            store(NG - 1)
            sp.wait_ge(sem["d_out"], 16 * NG)

        @block.gpsimd
        def _(pool):
            pool.memset(ident[:], 0.0).then_inc(sem["ident_set"], 1)
            pool.memset(blk[:], 0.0).then_inc(sem["ident_set"], 1)
            pool.wait_ge(sem["ident_set"], 2)
            pool.affine_select(out=ident[:], in_=ident[:], compare_op=ALU.not_equal, fill=1.0, base=0,
                               pattern=[[-1, 128]], channel_multiplier=1).then_inc(sem["ident_set"], 1)
            for h in range(2):
                pool.wait_ge(sem["ident_set"], 3 + h)
                pool.memset(blk[64 * h:64 * h + 64, 64 * h:64 * h + 64], 1.0).then_inc(sem["ident_set"], 1)
            pool.wait_ge(sem["ident_set"], 5)
            pool.iota(iota_i[:], [[1, T]], base=0, channel_multiplier=0).then_inc(sem["ident_set"], 1)
            pool.memset(tri[:], 1.0).then_inc(sem["ident_set"], 1)
            pool.wait_ge(sem["ident_set"], 7)
            pool.affine_select(out=tri[:], in_=tri[:], compare_op=ALU.is_ge, fill=0.0, base=-1,
                               pattern=[[1, 128]], channel_multiplier=-1).then_inc(sem["ident_set"], 1)
            pool.iota(tok[:], [[T, 2]], base=-GT, channel_multiplier=1).then_inc(sem["ident_set"], 1)
            pool.wait_ge(sem["disp_set"], 1)
            pool.dma_start(slots.rearrange("(p c) o -> p (c o)", p=128), no_nodes).then_inc(sem["slots_out"], 16)
            pool.wait_ge(sem["mx_all"], 1)
            pool.partition_all_reduce(ma[:, 0:6], mg[:, 0:6], 128, RMAX).then_inc(sem["mx_all"], 1)


            def tabs(i):
                for j in range(G):
                    pool.wait_ge(sem["ln_var"], 2 * i + j + 1)
                    pool.tensor_tensor(rs[:, j, :], vs[:, j, :], half[0:T, :], ALU.pow).then_inc(sem["ln_rs"], 1)
                for j in range(G):
                    pool.wait_ge(sem["xn_lo"], 2 * i + j + 1)
                    pool.dma_start(table[bass.ds(i * GT + j * T, T), :], tab[j]).then_inc(pair("tab_out")[j], 16)

            def sums(i):
                for j in range(G):
                    pool.wait_ge(sem["kf"], 2 * i + j + 1)
                    pool.wait_ge(sem["ksum_add"], 2 * i + j + 1)
                    pool.tensor_tensor(kacc, kacc, kf[j], ALU.add).then_inc(sem["ksum_add"], 1)

            def xt_store(i):
                for j in range(G):
                    pool.wait_ge(sem["xt_lo"], 2 * i + j + 1)
                pool.dma_start(xnt[bass.ds(i, 1), :, :].rearrange("a p n -> (a p) n"), xT.rearrange("p s k n -> p (s k n)")).then_inc(sem["xt_out"], 16)

            pool.wait_ge(sem["w_conv_hi"], NW + 1)
            pool.wait_ge(sem["w_conv_lo"], NW + 1)
            pool.dma_start(yd[MINS * CH:MAXS * CH, :].rearrange("(p r) (h n) -> p (r h) n", p=128, h=2),
                           no_nodes.bitcast(F32)[:, None, 0:D // 2].broadcast_to([128, (MAXS - MINS) * CH // 128 * 2, D // 2])).then_inc(sem["slots_out"], 16)
            pool.memset(kacc, 0.0).then_inc(sem["ksum_add"], 1)
            tabs(0)
            xt_store(0)
            with pool.Fori(0, NG - 1) as i:
                tabs(i + 1)
                sums(i)
                xt_store(i + 1)
            sums(NG - 1)
            for j in range(G):
                pool.wait_ge(pair("tab_out")[j], 16 * NG)
            pool.wait_ge(sem["xt_out"], 16 * NG)
            pool.wait_ge(sem["ctx_ps"], 2 * NG + 1)
            pool.wait_ge(sem["ksum_ps"], 1)

            def gathers(g, j):
                t = 2 * g + j
                lo = pool.value_load(sched[0:1, 1, bass.ds(t, 1)], min_val=0, max_val=4000)
                hi = pool.value_load(sched[0:1, 1, bass.ds(t + 1, 1)], min_val=1, max_val=4000)
                with pool.Fori(lo, hi) as r:
                    edges_in, rows_free = pool.to_reg((r + 1) * 16), pool.to_reg(r + 1)
                    pool.wait_ge(sem["consts"], 1)
                    pool.wait_ge(sem["e_in"], edges_in)
                    pool.wait_ge(sem["agg_half"], rows_free)
                    for s in range(SPLIT):
                        pool.indirect_dma_start(
                            out=ring[:, s, :], out_offset=None, in_=table,
                            in_offset=bass.IndirectOffsetOnAxis(ap=ebuf[j][:, 2 * s:2 * s + 1].bitcast(U32), axis=0),
                        ).then_inc(sem["gathered_a"], 16)
                    pool.wait_ge(sem["consts"], 1)
                    pool.wait_ge(sem["agg_ps"], rows_free)
                    for s in range(SPLIT, SLOTS):
                        pool.indirect_dma_start(
                            out=ring[:, s, :], out_offset=None, in_=table,
                            in_offset=bass.IndirectOffsetOnAxis(ap=ebuf[j][:, 2 * s:2 * s + 1].bitcast(U32), axis=0),
                        ).then_inc(sem["gathered_b"], 16)

            def dispatch(i):
                placed_in = of(pool, GATE_STEPS * i + 17)
                pool.wait_ge(sem["consts"], 1)
                pool.wait_ge(sem["gate_dve"], placed_in)
                for j in range(G):
                    for k in range(2):
                        pool.indirect_dma_start(
                            out=slots, out_offset=bass.IndirectOffsetOnAxis(ap=posi[:, j, k:k + 1].bitcast(U32), axis=0),
                            in_=tok[:, j:j + 1], in_offset=None,
                        ).then_inc(sem["scat"], 16)

            def residual(i):
                pool.wait_ge(sem["xg_in"], 16 * (i + 1))
                pool.tensor_tensor(xg, xg, beta_bc[0:T, None, :].broadcast_to([T, G, D]), ALU.add).then_inc(sem["xb"], 1)

            pool.wait_ge(sem["sched_set"], 1)
            gathers(0, 0)
            pool.wait_ge(sem["mf_max"], 1)
            pool.partition_all_reduce(ma[:, 6:7], mg[:, 6:7], 128, RMAX).then_inc(sem["mh_all"], 1)
            gathers(0, 1)
            pool.wait_ge(sem["slots_out"], 32)
            pool.wait_ge(sem["beta_set"], 1)
            residual(0)
            gathers(1, 0)
            gathers(1, 1)
            residual(1)
            gathers(2, 0)
            gathers(2, 1)
            with pool.Fori(2, NG - 1) as i:
                residual(i)
                gathers(i + 1, 0)
                dispatch(i - 2)
                gathers(i + 1, 1)
            residual(NG - 1)
            dispatch(NG - 3)
            dispatch(NG - 2)
            dispatch(NG - 1)

            pool.wait_ge(sem["agg_end"], NT)
            pool.wait_ge(sem["rows2_out"], 16 * NG)

            def rows_of(r):
                rows_free = of(pool, 2 * r)
                pool.wait_ge(sem["consts"], 1)
                if past(r):
                    pool.wait_ge(sem["ct_ps"], rows_free)
                for c in range(2):
                    pool.indirect_dma_start(
                        out=tg[:, c, :], out_offset=None, in_=table2,
                        in_offset=bass.IndirectOffsetOnAxis(ap=idx[:, c:c + 1].bitcast(U32), axis=0),
                    ).then_inc(sem["g_in"], 16)

            pool.wait_ge(sem["sched2_set"], 1)
            total = pool.value_load(sched2[0:1, NE:NE + 1], min_val=2 * NE, max_val=400)
            pool.wait_ge(sem["ix_in"], 16)
            rows_of(0)
            with pool.Fori(1, total) as r:
                list_in = pool.to_reg((r + 1) * 16)
                pool.wait_ge(sem["consts"], 1)
                pool.wait_ge(sem["ix_in"], list_in)
                rows_of(r)
            rows_of(total)

            all_out = pool.to_reg(total * 16 + 16)
            pool.wait_ge(sem["consts"], 1)
            pool.wait_ge(sem["y_st"], all_out)
            pool.wait_ge(sem["x2_out"], 16 * NG)
            pool.wait_ge(sem["x2t_out"], 16 * NG)

            def chosen_rows(i):
                if past(i):
                    pool.wait_ge(sem["yg_in"], 64 * i)
                    pool.wait_ge(sem["d_y"], 4 * i)
                pool.tensor_copy(yi[:], pos[:, bass.ds(2 * i, 2), :].rearrange("p j k -> p (j k)")).then_inc(sem["yi_set"], 1)
                pool.tensor_copy(wcur[:], wk[:, bass.ds(2 * i, 2), :].rearrange("p j k -> p (j k)")).then_inc(sem["yi_set"], 1)
                slots_in = of(pool, 2 * i + 2)
                pool.wait_ge(sem["consts"], 1)
                pool.wait_ge(sem["yi_set"], slots_in)
                for j in range(G):
                    for k in range(2):
                        pool.indirect_dma_start(
                            out=yr[:, j, k, :], out_offset=None, in_=yd,
                            in_offset=bass.IndirectOffsetOnAxis(ap=yi[:, 2 * j + k:2 * j + k + 1].bitcast(U32), axis=0),
                        ).then_inc(sem["yg_in"], 16)

            pool.wait_ge(sem["yd_pos"], 1)
            chosen_rows(0)
            with pool.Fori(1, NG) as i:
                chosen_rows(i)

        @block.scalar
        def _(act):
            act.wait_ge(sem["mx_scale"], 5)
            for n in order:
                _, held, dst, grp, _ = wlist[n]
                if n > FF:
                    act.wait_ge(sem["w_conv_hi"], order.index(n - 1) + 1)
                    act.wait_ge(sem["w_conv_lo"], order.index(n - 1) + 1)
                act.activation(dst[:, 0, :], held, ACT.Copy, scale=sg[:, grp:grp + 1]).then_inc(sem["w_conv_hi"], 1)
            act.activation(Wg[:, 0].rearrange("p k n -> p (k n)"), wgf[:], ACT.Copy, scale=sg[:, GW:GW + 1]).then_inc(sem["w_conv_hi"], 1)

            def hi(i):
                for j in range(G):
                    act.wait_ge(sem["ln_out"], 2 * i + j + 1)
                    if past(i):
                        act.wait_ge(pair("tab_out")[j], 16 * i)
                    act.activation(tab[j][:, 0:D], xn[j], ACT.Copy).then_inc(sem["xn_hi"], 1)

            def features(i):
                for j in range(G):
                    act.wait_ge(sem["k_neg"], 2 * i + j + 1)
                    if past(i):
                        act.wait_ge(sem["kf"], 2 * i + j - 1)
                    act.activation(kr[j], bank[2 + j][0:T, :], ACT.Relu, scale=sv[0:T, S_KV:S_KV + 1]).then_inc(sem["k_relu"], 1)
                    act.activation(ke[j], ke[j], ACT.Exp).then_inc(sem["k_exp"], 1)
                    act.wait_ge(sem["v_ps"], 2 * i + j + 1)
                    act.wait_ge(sem["ctx_ps"], 2 * i + 1)
                    act.activation(vf[j], bank[4 + j][0:T, :], ACT.Copy, scale=sv[0:T, S_KV:S_KV + 1]).then_inc(sem["v_sb"], 1)

            def hi_t(i):
                for j in range(G):
                    act.wait_ge(sem["xt_ps"], 2 * i + j + 1)
                    if past(i):
                        act.wait_ge(sem["v_ps"], 2 * i + j - 1)
                    if past(i):
                        act.wait_ge(sem["xt_out"], 16 * i)
                    act.activation(xT[:, 0, :, both(j)], four(j), ACT.Copy).then_inc(sem["xt_hi"], 1)

            hi(0)
            hi_t(0)
            hi(1)
            features(0)
            hi_t(1)
            with act.Fori(1, NG - 1) as i:
                hi(i + 1)
                features(i)
                hi_t(i + 1)
            features(NG - 1)

            act.wait_ge(sem["mh_scale"], 5)
            act.activation(Mh[:, 0].rearrange("p k n -> p (k n)"), Mf.rearrange("p k n -> p (k n)"), ACT.Copy, scale=sg[:, MH:MH + 1]).then_inc(sem["mh_hi"], 1)
            act.wait_ge(sem["mh_done"], 1)

            def split_normalised(i):
                for j in range(G):
                    act.wait_ge(sem["tn_sb"], 2 * i + j + 1)
                    if past(i):
                        act.wait_ge(sem["rows2_out"], 16 * i)
                        act.wait_ge(sem["tt_ps"], 2 * i)
                    act.activation(tab2[:, j, 0:D], tn[:, j, :], ACT.Copy).then_inc(sem["tn_hi"], 1)

            def turned(i):
                for j in range(G):
                    act.wait_ge(sem["tt_ps"], 2 * i + j + 1)
                    if past(i):
                        act.wait_ge(sem["gate_ps"], 2 * i)
                        act.wait_ge(sem["x2t_out"], 16 * i)
                    act.activation(tT[:, :, :, both(j)], parts16(j, T), ACT.Copy).then_inc(sem["tt_sb"], 1)

            def gate(i):
                act.wait_ge(sem["gate_dve"], GATE_STEPS * i + 6)
                if past(i):
                    act.wait_ge(sem["gate_dve"], GATE_STEPS * (i - 1) + 11)
                for j in range(G):
                    act.activation(ge[:, j, :], gl[:, j, :], ACT.Exp, bias=gs[:, j, 0:1], accum_out=gs[:, j, 1:2]).then_inc(sem["gate_exp"], 1)
                    act.activation(ew[:, j, :], g8[:, j, 0:2], ACT.Exp, bias=gs[:, j, 0:1]).then_inc(sem["gate_exp"], 1)

            def group(i, prev):
                for c in range(2):
                    cc = slice(2 * c, 2 * c + 2)
                    act.wait_ge(sem["q_neg"], 2 * i + c + 1)
                    if past(i):
                        act.wait_ge(sem["x2_sb"], 2 * i)
                    act.activation(qr[:, cc, :], two(4 + c), ACT.Relu, scale=sv[:, S_Q:S_Q + 1]).then_inc(sem["q_relu"], 1)
                    if c == 0:
                        act.activation(qe[:, cc, :], qe[:, cc, :], ACT.Exp).then_inc(sem["q_exp"], 1)
                for j in range(G):
                    act.wait_ge(sem["mt_ps"], 2 * i + j + 1)
                    if past(i):
                        act.wait_ge(sem["h_ps"], 2 * i)
                    act.activation(mT[:, 0, :, both(j)], four(2 + j), ACT.Copy).then_inc(sem["mt_hi"], 1)
                act.activation(qe[:, 2:4, :], qe[:, 2:4, :], ACT.Exp).then_inc(sem["q_exp"], 1)
                if prev is not None:
                    split_normalised(prev)
                for c in range(2):
                    act.wait_ge(sem["q_phi"], 2 * i + c + 1)
                    for k in (2 * c, 2 * c + 1):
                        act.activation(qe[:, k, :], qe[:, k, :], ACT.Copy, scale=ksum[:, k:k + 1]).then_inc(sem["q_u"], 1)
                if prev is not None:
                    turned(prev)
                for c in range(2):
                    act.wait_ge(sem["den_ps"], 2 * i + c + 1)
                    act.activation(qr[:, 2 * c:2 * c + 2, :], two(c), ACT.Identity, bias=tiny[:]).then_inc(sem["q_den"], 1)
                for c in range(2):
                    act.wait_ge(sem["q_hat"], 2 * i + c + 1)
                    if past(i):
                        act.wait_ge(sem["att_ps"], 2 * i)
                    act.activation(qh[:, 0, 2 * c:2 * c + 2, :], qe[:, 2 * c:2 * c + 2, :], ACT.Copy).then_inc(sem["q_hi"], 1)
                if prev is not None:
                    gate(prev)

            group(0, None)
            group(1, 0)
            with act.Fori(2, NG) as i:
                group(i, i - 1)
            split_normalised(NG - 1)
            turned(NG - 1)
            gate(NG - 1)

            act.wait_ge(sem["agg_end"], NT)
            act.wait_ge(sem["sched2_set"], 1)

            def turned_rows(r):
                act.wait_ge(sem["ct_ps"], 2 * r + 1)
                if past(r):
                    act.wait_ge(sem["ch_ps"], r)
                act.activation(tTc[:, :, :, 0:128], parts16(2, 128), ACT.Copy).then_inc(sem["ct_act"], 1)

            def step(e, r):
                act.wait_ge(sem["ch_ps"], r + 1)
                if past(r):
                    act.wait_ge(sem["c_lo"], r)
                for c in range(2):
                    f = 2 * (NS + e) + c
                    act.activation(gelc[:, c, :], bank[0][:, c * CH:(c + 1) * CH], ACT.Gelu, bias=b1[:, f:f + 1],
                                   scale=sv[:, S_W1:S_W1 + 1]).then_inc(sem["c_gelu"], 1)
                turned_rows(r + 1)
                act.wait_ge(sem["c_gelu"], 2 * r + 2)
                if past(r):
                    act.wait_ge(sem["cp_ps"], 2 * r + 1)
                act.activation(hTc[:, 0], gelc, ACT.Copy, scale=sg[:, HB:HB + 1]).then_inc(sem["c_hi"], 1)

            def store_rows(n):
                act.wait_ge(sem["y_sb"], 2 * n + 3)
                off = nc.s_assert_within((n - 1) * CH, 0, (MAXS - 1) * CH,
                                          skip_runtime_bounds_check_because="there are no more than MAXS steps")
                act.dma_start(yd[bass.ds(off, CH), :].rearrange("(p c) n -> p c n", p=128), ysb).then_inc(sem["y_st"], 16)

            turned_rows(0)
            for e in range(NE):
                lo = act.value_load(sched2[0:1, e:e + 1], min_val=2 * e, max_val=400) if e else 0
                hi = act.value_load(sched2[0:1, e + 1:e + 2], min_val=2 * e + 2, max_val=400)
                step(e, lo)
                if e:
                    store_rows(lo)
                with act.Fori(lo + 1, hi) as r:
                    step(e, r)
                    store_rows(r)
            store_rows(hi)

            def shared(i):
                for e in range(NS):
                    act.wait_ge(sem["d_f1"], 2 * i + e + 1)
                    if past(i):
                        act.wait_ge(sem["d_lo"], 2 * i + e - 1)
                    for c in range(2):
                        f = 2 * e + c
                        act.activation(geld[e][:, c, :], two(e)[:, c, :], ACT.Gelu, bias=b1[:, f:f + 1],
                                       scale=sv[:, S_W1:S_W1 + 1]).then_inc(sem["d_gelu"], 1)
                    act.wait_ge(sem["d_gelu"], 4 * i + 2 * e + 2)
                    if past(i):
                        act.wait_ge(sem["d_f2"], 2 * i)
                    act.activation(hTd[e][:, 0], geld[e], ACT.Copy, scale=sg[:, HB:HB + 1]).then_inc(sem["d_hi"], 1)

            act.wait_ge(sem["x2_out"], 16 * NG)
            act.wait_ge(sem["rows2_out"], 16 * NG)
            act.wait_ge(sem["x2t_out"], 16 * NG)
            shared(0)
            with act.Fori(1, NG) as i:
                shared(i)

        @block.tensor
        def _(pe):
            pe.wait_ge(sem["consts"], 8)
            pe.wait_ge(sem["ident_set"], 6)
            wmm(bank[6][:, :], zeros16[0:1, 0:128], zeros16[0:1, :], start=True, stop=False, skip_group_check=True).then_inc(sem["ctx_ps"], 1)
            pe.wait_ge(sem["w_conv_hi"], NW + 1)
            pe.wait_ge(sem["w_conv_lo"], NW + 1)

            for name, start in (("ring_in", 1), ("agg_half", 1), ("agg_ps", 1), ("cp_ps", 1), ("y_sb", 3), ("y_st", 16)):
                pe.nop().then_inc(sem[name], start)

            def turn(i):
                for j in range(G):
                    pe.wait_ge(sem["ln_out"], 2 * i + j + 1)
                    if past(i):
                        pe.wait_ge(sem["xt_lo"], 2 * i + j - 1)
                    for k in range(KC):
                        last = pe.transpose(four(j)[:, k, :], xn[j][:, k * 128:(k + 1) * 128], ident[0:T, 0:T])
                    last.then_inc(sem["xt_ps"], 1)

            def keys_values(i):
                for j in range(G):
                    pe.wait_ge(sem["xt_hi"], 2 * i + j + 1)
                    pe.wait_ge(sem["xt_lo"], 2 * i + j + 1)
                    if past(i):
                        pe.wait_ge(sem["k_neg"], 2 * i + j - 1)
                    for b, done, used in ((2, "k_ps", "k_relu"), (4, "v_ps", "v_sb")):
                        if past(i):
                            pe.wait_ge(sem[used], 2 * i + j - 1)
                        w0 = 0 if b == 2 else D
                        for k in range(KC):
                            last = three(bank[b + j][0:T, :], xT[:, 0, k, both(j)], xT[:, 1, k, both(j)],
                                         Wkv[:, 0, k, w0:w0 + D], Wkv[:, 1, k, w0:w0 + D], k == 0, k == KC - 1)
                        last.then_inc(sem[done], 1)

            def context(i):
                for j in range(G):
                    pe.wait_ge(sem["kf"], 2 * i + j + 1)
                    pe.wait_ge(sem["v_sb"], 2 * i + j + 1)
                    for p in range(KC):
                        c = slice(128 * p, 128 * p + 128)
                        last = wmm(bank[6][:, c], vf[j][:, c], kf[j][:, c], start=False, stop=False, skip_group_check=True)
                    last.then_inc(sem["ctx_ps"], 1)

            turn(0)
            keys_values(0)
            turn(1)
            context(0)
            with pe.Fori(1, NG - 1) as i:
                keys_values(i)
                turn(i + 1)
                context(i)
            keys_values(NG - 1)
            context(NG - 1)

            pe.wait_ge(sem["edge_cnt"], NT)
            pe.wait_ge(sem["v_sb"], 2 * NG)
            wmm(bank[5][0:1, 0:52], ones[0:EP, :], cnt[0:EP, 0:52], start=True, stop=True).then_inc(sem["edge_sum"], 1)
            pe.wait_ge(sem["ksum_add"], 2 * NG + 1)
            for p in range(KC):
                last = wmm(bank[7][:, p:p + 1], kacc[:, 128 * p:128 * p + 128], ones[0:T, :], start=(p == 0), stop=True, skip_group_check=True)
            last.then_inc(sem["ksum_ps"], 1)
            pe.wait_ge(sem["ctx_sb"], 1)
            pe.wait_ge(sem["wout_in"], 32)
            for p in range(KC):
                wmm(bank[p][:, :], ctxT[:, p, :], WoutT[:, p, :], start=True, stop=True).then_inc(sem["m_ps"], 1)

            def aggregate(g, j):
                t = 2 * g + j
                lo = pe.value_load(sched[0:1, 1, bass.ds(t, 1)], min_val=0, max_val=4000)
                hi = pe.value_load(sched[0:1, 1, bass.ds(t + 1, 1)], min_val=1, max_val=4000)
                if past(t):
                    pe.wait_ge(sem["mean_sb"], t)
                wmm(bank[6][0:T, :], zeros16[0:1, 0:T], zeros16[0:1, :], start=True, stop=False, skip_group_check=True)
                wmm(bank[7][0:T, 0:1], zeros16[0:1, 0:T], zeros16[0:1, 0:1], start=True, stop=False, skip_group_check=True)
                with pe.Fori(lo, hi) as r:
                    pe.wait_ge(sem["onehot_cnt"], r + 1)
                    wmm(bank[7][0:T, 0:1], ohc[:], ones16[:], start=False, stop=False, skip_group_check=True)
                    pe.wait_ge(sem["gathered_a"], (r + 1) * (16 * SPLIT))
                    for s in range(SLOTS):
                        if s == SPLIT:
                            pe.wait_ge(sem["gathered_b"], (r + 1) * (16 * (SLOTS - SPLIT)))
                        for part in range(2):
                            last = wmm(bank[6][0:T, :], oh[:, s, :], ring[:, s, part * D:(part + 1) * D],
                                       start=False, stop=False, skip_group_check=True)
                            if s == SPLIT and part == 0:
                                last.then_inc(sem["ring_in"], 1)
                        if s == SPLIT - 1:
                            last.then_inc(sem["agg_half"], 1)
                    last.then_inc(sem["agg_ps"], 1)
                wmm(bank[6][0:T, 0:1], zeros16[0:1, 0:T], zeros16[0:1, 0:1], start=False, stop=True, skip_group_check=True).then_inc(sem["agg_end"], 1)

            def turn_normalised(i):
                for j in range(G):
                    pe.wait_ge(sem["tn_hi"], 2 * i + j + 1)
                    pe.wait_ge(sem["tn_lo"], 2 * i + j + 1)
                    pe.wait_ge(sem["x2_sb"], 2 * i + j + 1)
                    for part in range(2):
                        for k in range(KC):
                            c = part * D + k * 128
                            last = pe.transpose(parts16(j, T)[:, part, k, :], tab2[:, j, c:c + 128], ident16[0:T, 0:T])
                    last.then_inc(sem["tt_ps"], 1)

            def gate(i):
                pe.wait_ge(sem["tt_sb"], 2 * i + 2)
                for j in range(G):
                    for k in range(KC):
                        last = three(bank[2][0:T, 8 * j:8 + 8 * j], tT[:, 0, k, both(j)], tT[:, 1, k, both(j)],
                                     Wg[:, 0, k, :], Wg[:, 1, k, :], k == 0, k == KC - 1)
                    last.then_inc(sem["gate_ps"], 1)

            def places(i):
                pe.wait_ge(sem["gate_dve"], GATE_STEPS * i + 9)
                for j in range(G):
                    ps = bank[3][0:T, 8 * j:8 + 8 * j]
                    wmm(ps, tri16[0:T, 0:T], chosen[:, j, :], start=True, stop=False)
                    if j:
                        wmm(ps, ones16w[0:T, 0:T], chosen[:, 0, :], start=False, stop=False)
                    last = wmm(ps, ones16w[0:T, 0:T], before[:], start=False, stop=True)
                last.then_inc(sem["pos_ps"], 1)

            def group(i, prev, nxt):
                pe.wait_ge(sem["xt_in"], 16 * (i + 1))
                if past(i):
                    pe.wait_ge(sem["h_sb"], 2 * i)
                for c in range(KC):
                    for k in range(KC):
                        f = slice(128 * c, 128 * c + 128)
                        ps = two(4 + c // 2)[:, c % 2, :]
                        wmm(ps, Wq[:, 0, k, f], xTg[:, 0, k, :], start=(k == 0), stop=False)
                        wmm(ps, Wq[:, 0, k, f], xTg[:, 1, k, :], start=False, stop=False)
                        last = wmm(ps, Wq[:, 1, k, f], xTg[:, 0, k, :], start=False, stop=(k == KC - 1))
                    if c % 2:
                        last.then_inc(sem["q_ps"], 1)
                if prev is not None and past(prev):
                    pe.wait_ge(sem["gate_dve"], GATE_STEPS * (prev - 1) + 12)
                for j in range(G):
                    pe.wait_ge(sem["mean_sb"], 2 * i + j + 1)
                    for k in range(KC):
                        last = pe.transpose(four(2 + j)[:, k, :], mean[:, j, k * 128:(k + 1) * 128], ident[0:T, 0:T])
                    last.then_inc(sem["mt_ps"], 1)
                for j in range(G):
                    pe.wait_ge(sem["q_relu"], 2 * i + j + 1)
                    pe.wait_ge(sem["q_neg"], 2 * i + j + 1)
                    for k in range(KC):
                        three(bank[4 + j][0:T, :], xTg[:, 0, k, both(j)], xTg[:, 1, k, both(j)],
                              Wsn[:, 0, k, :], Wsn[:, 1, k, :], k == 0, False)
                    pe.wait_ge(sem["mt_hi"], 2 * i + j + 1)
                    pe.wait_ge(sem["mt_lo"], 2 * i + j + 1)
                    for k in range(KC):
                        last = three(bank[4 + j][0:T, :], mT[:, 0, k, both(j)], mT[:, 1, k, both(j)],
                                     Wsn[:, 0, KC + k, :], Wsn[:, 1, KC + k, :], False, k == KC - 1)
                    last.then_inc(sem["h_ps"], 1)
                    if j == 0:
                        if prev is not None:
                            turn_normalised(prev)
                            pe.wait_ge(sem["tt_sb"], 2 * prev + 2)
                        for c in range(2):
                            pe.wait_ge(sem["q_u"], 4 * i + 2 * c + 2)
                            for k in range(2):
                                last = wmm(two(c)[:, k, :], blk[:], qe[:, 2 * c + k, :], start=True, stop=True)
                            last.then_inc(sem["den_ps"], 1)
                        if nxt is not None:
                            aggregate(nxt, 0)
                        if prev is not None:
                            pe.wait_ge(sem["mt_lo"], 2 * i + 2)
                            gate(prev)
                pe.wait_ge(sem["mh_done"], 1)
                pe.wait_ge(sem["q_hi"], 2 * i + 2)
                pe.wait_ge(sem["q_lo"], 2 * i + 2)
                for j in range(G):
                    for k in range(KC):
                        last = three(bank[j][0:T, :], qh[:, 0, k, both(j)], qh[:, 1, k, both(j)],
                                     Mh[:, 0, k, :], Mh[:, 1, k, :], k == 0, k == KC - 1)
                    last.then_inc(sem["att_ps"], 1)
                if prev is not None:
                    places(prev)
                if nxt is not None:
                    aggregate(nxt, 1)

            pe.wait_ge(sem["sched_set"], 1)
            pe.wait_ge(sem["ksum_sb"], 1)
            pe.wait_ge(sem["mf_set"], KC)
            aggregate(0, 0)
            aggregate(0, 1)
            group(0, None, 1)
            group(1, 0, 2)
            with pe.Fori(2, NG - 1) as i:
                group(i, i - 1, i + 1)
            group(NG - 1, NG - 2, None)
            turn_normalised(NG - 1)
            pe.wait_ge(sem["gate_dve"], GATE_STEPS * (NG - 2) + 12)
            gate(NG - 1)
            places(NG - 1)
            pe.wait_ge(sem["gate_dve"], GATE_STEPS * NG)
            wmm(bank[2][0:T, 0:NE], ones16w[0:T, 0:T], before[:], start=True, stop=True).then_inc(sem["cnt_ps"], 1)

            pe.wait_ge(sem["sched2_set"], 1)

            def turn_rows(r):
                pe.wait_ge(sem["g_in"], (r + 1) * 32)
                if past(r):
                    pe.wait_ge(sem["ct_act"], r)
                    pe.wait_ge(sem["ct_dve"], r)
                for c in range(2):
                    for part in range(2):
                        for k in range(KC):
                            f = part * D + k * 128
                            last = pe.transpose(parts16(2 + c, 128)[:, part, k, :], tg[:, c, f:f + 128], ident16[:, :])
                    last.then_inc(sem["ct_ps"], 1)

            def hidden(e, r):
                pe.wait_ge(sem["ct_act"], r + 1)
                pe.wait_ge(sem["ct_dve"], r + 1)
                if past(r):
                    pe.wait_ge(sem["c_gelu"], 2 * r)
                for c in range(2):
                    f = slice(256 * (NS + e) + 128 * c, 256 * (NS + e) + 128 * c + 128)
                    ps = bank[0][:, c * CH:(c + 1) * CH]
                    for k in range(KC):
                        wmm(ps, w1(0, k, f), tTc[:, 0, k, :], start=(k == 0), stop=False)
                        wmm(ps, w1(0, k, f), tTc[:, 1, k, :], start=False, stop=False)
                        last = wmm(ps, w1(1, k, f), tTc[:, 0, k, :], start=False, stop=(k == KC - 1))
                last.then_inc(sem["ch_ps"], 1)

            def project(e, n):
                pe.wait_ge(sem["c_hi"], n)
                pe.wait_ge(sem["c_lo"], n)
                for j in range(2):
                    pe.wait_ge(sem["y_sb"], 2 * n + j)
                    for c in range(2):
                        f = 2 * (NS + e) + c
                        m = slice(128 * j, 128 * j + 128)
                        last = three(bank[4 + j][:, :], hTc[:, 0, c, m], hTc[:, 1, c, m],
                                     w2(0, f), w2(1, f), c == 0, c == 1)
                    last.then_inc(sem["cp_ps"], 1)

            turn_rows(0)
            for e in range(NE):
                lo = pe.value_load(sched2[0:1, e:e + 1], min_val=2 * e, max_val=400) if e else 0
                hi = pe.value_load(sched2[0:1, e + 1:e + 2], min_val=2 * e + 2, max_val=400)
                hidden(e, lo)
                turn_rows(lo + 1)
                if e:
                    project(e - 1, lo)
                with pe.Fori(lo + 1, hi) as r:
                    hidden(e, r)
                    turn_rows(r + 1)
                    project(e, r)
            project(NE - 1, hi)

            def hidden_shared(i, b, e):
                if e == 0:
                    pe.wait_ge(pair("dt_in")[b], 8 * (i + 2) if b == 0 else 8 * (i + 1))
                if past(i):
                    pe.wait_ge(sem["d_gelu"], 4 * i - 2 + 2 * e)
                for c in range(2):
                    f = slice(256 * e + 128 * c, 256 * e + 128 * c + 128)
                    ps = two(e)[:, c, :]
                    for k in range(KC):
                        wmm(ps, w1(0, k, f), tTd[b][:, 0, k, :], start=(k == 0), stop=False)
                        wmm(ps, w1(0, k, f), tTd[b][:, 1, k, :], start=False, stop=False)
                        last = wmm(ps, w1(1, k, f), tTd[b][:, 0, k, :], start=False, stop=(k == KC - 1))
                last.then_inc(sem["d_f1"], 1)

            def project_shared(i, e):
                pe.wait_ge(sem["d_hi"], 2 * i + e + 1)
                pe.wait_ge(sem["d_lo"], 2 * i + e + 1)
                for j in range(G):
                    if past(i) and e == 0:
                        pe.wait_ge(sem["d_res"], 2 * i + j - 1)
                    for c in range(2):
                        f = 2 * e + c
                        last = three(bank[2 + j][0:T, :], hTd[e][:, 0, c, both(j)], hTd[e][:, 1, c, both(j)],
                                     w2(0, f), w2(1, f), f == 0, f == 2 * NS - 1)
                    if e == NS - 1:
                        last.then_inc(sem["d_f2"], 1)

            last_rows = pe.value_load(sched2[0:1, NE:NE + 1], min_val=2 * NE, max_val=400)
            pe.wait_ge(sem["ct_act"], last_rows + 1)
            pe.wait_ge(sem["ct_dve"], last_rows + 1)
            pe.wait_ge(sem["c_gelu"], 2 * last_rows)
            hidden_shared(0, 0, 0)
            hidden_shared(0, 0, 1)
            project_shared(0, 0)
            with pe.Fori(0, (NG - 1) // 2) as m:
                for b in (1, 0):
                    i = 2 * m + 2 - b
                    hidden_shared(i, b, 0)
                    project_shared(i - 1, 1)
                    hidden_shared(i, b, 1)
                    project_shared(i, 0)
            project_shared(NG - 1, 1)

        @block.vector
        def _(dve):
            tt, ts, stt = dve.tensor_tensor, dve.tensor_scalar, dve.scalar_tensor_tensor
            for t, v in ((ones, 1.0), (ones16, 1.0), (half, -0.5), (tiny, 1e-8), (zeros16, 0.0), (ones16w, 1.0), (mx, 0.0), (before, 0.0)):
                dve.memset(t[:], v).then_inc(sem["consts"], 1)
            dve.memset(no_nodes, 0).then_inc(sem["disp_set"], 1)
            dve.wait_ge(sem["ident_set"], 6)
            dve.tensor_copy(iota_f[:], iota_i[:]).then_inc(sem["iota_set"], 1)
            dve.wait_ge(sem["iota_set"], 1)
            dve.tensor_copy(iota_e[:], iota_f[:, 0:NE]).then_inc(sem["iota_set"], 1)
            dve.wait_ge(sem["iota_set"], 2)
            ts(eoff[:], iota_e[:], float(CAP), None, ALU.mult).then_inc(sem["disp_set"], 1)
            dve.wait_ge(sem["ident_set"], 9)
            dve.tensor_copy(ident16[:], ident[:]).then_inc(sem["disp_set"], 1)
            dve.tensor_copy(tri16[:], tri[:]).then_inc(sem["disp_set"], 1)
            ts(thr[:, 0:NT + 1], iota_f[:, 0:NT + 1], float(T), None, ALU.mult).then_inc(sem["iota_set"], 1)
            dve.wait_ge(sem["dst_in"], 32)
            dve.tensor_copy(d_f[0:EP, :], d_i[0:EP, :]).then_inc(sem["edge_cast"], 1)
            dve.memset(cnt[0:EP, :], 0.0).then_inc(sem["edge_cast"], 1)
            dve.wait_ge(sem["edge_cast"], 2)
            dve.wait_ge(sem["iota_set"], 3)
            tt(junk[0:EP, :], d_i[0:EP, :], n_i[0:EP, :], ALU.is_gt).then_inc(sem["edge_viol"], 1)
            dve.wait_ge(sem["edge_viol"], 1)
            dve.tensor_reduce(cnt[0:EP, 51:52], junk[0:EP, :], AX_X, ALU.add).then_inc(sem["edge_viol"], 1)
            dve.wait_ge(sem["edge_viol"], 2)
            for n, (_, held, _, grp, loaded) in enumerate(wlist):
                dve.wait_ge(sem[loaded], 16 * sum(w[3] == grp for w in wlist))
                dve.tensor_reduce(mx[:, n:n + 1], held, AX_X, ALU.max, apply_absolute_value=True).then_inc(sem["mx_done"], 1)
            dve.wait_ge(sem["small_in"], 48)
            dve.tensor_reduce(mg[:, GW:GW + 1], wgf[:], AX_X, ALU.max, apply_absolute_value=True).then_inc(sem["mx_done"], 1)
            dve.tensor_reduce(mg[:, HB:HB + 1], b1[:], AX_X, ALU.max, apply_absolute_value=True).then_inc(sem["mx_done"], 1)
            dve.wait_ge(sem["mx_done"], NW + 2)
            n0 = 0
            for grp in (KVQ, SN, W1, W2):
                n1 = n0 + sum(w[3] == grp for w in wlist)
                r = dve.tensor_reduce(mg[:, grp:grp + 1], mx[:, n0:n1], AX_X, ALU.max)
                n0 = n1
                r.then_inc(sem["mx_done"], 1)
            dve.wait_ge(sem["mx_done"], NW + 6)
            dve.memset(mg[:, 7:8], 0.0).then_inc(sem["mx_all"], 1)
            dve.wait_ge(sem["mx_all"], 2)

            def scales(c0, c1, sm, n):
                ts(ma[:, c0:c1], ma[:, c0:c1], 2.0 ** -40, None, ALU.max).then_inc(sm, 1)
                dve.wait_ge(sm, n + 1)
                ts(mp[:, c0:c1].bitcast(I32), ma[:, c0:c1].bitcast(I32), 0x7F800000, None, ALU.bitwise_and).then_inc(sm, 1)
                dve.wait_ge(sm, n + 2)
                ts(sg[:, c0:c1].bitcast(I32), mp[:, c0:c1].bitcast(I32), -1.0, float((127 + 14 + 127) << 23), ALU.mult, ALU.add).then_inc(sm, 1)
                dve.wait_ge(sm, n + 3)
                ts(si[:, c0:c1].bitcast(I32), sg[:, c0:c1].bitcast(I32), -1.0, float(254 << 23), ALU.mult, ALU.add).then_inc(sm, 1)
                dve.wait_ge(sm, n + 4)

            stt(ma[:, HB:HB + 1], ma[:, W1:W1 + 1], 512.0, ma[:, HB:HB + 1], ALU.mult, ALU.add).then_inc(sem["mx_scale"], 1)
            dve.wait_ge(sem["mx_scale"], 1)
            scales(0, 6, sem["mx_scale"], 1)
            for col, grp, f in ((S_KV, KVQ, 1 / XS), (S_Q, KVQ, 1 / (8 * XS)), (S_H, SN, 1 / XS), (S_W1, W1, 1 / XS), (S_G, GW, 1 / XS)):
                ts(sv[:, col:col + 1], si[:, grp:grp + 1], f, None, ALU.mult).then_inc(sem["mx_scale"], 1)
            tt(sv[:, S_W2:S_W2 + 1], si[:, W2:W2 + 1], si[:, HB:HB + 1], ALU.mult).then_inc(sem["mx_scale"], 1)
            for step, n in enumerate(order):
                _, held, dst, grp, _ = wlist[n]
                dve.wait_ge(sem["w_conv_hi"], step + 1)
                stt(dst[:, 1, :], held, sg[:, grp:grp + 1], dst[:, 0, :], ALU.mult, ALU.subtract).then_inc(sem["w_conv_lo"], 1)
            dve.wait_ge(sem["w_conv_hi"], NW + 1)
            stt(Wg[:, 1].rearrange("p k n -> p (k n)"), wgf[:], sg[:, GW:GW + 1], Wg[:, 0].rearrange("p k n -> p (k n)"),
                ALU.mult, ALU.subtract).then_inc(sem["w_conv_lo"], 1)

            def statistics(i, src):
                for j in range(G):
                    dve.wait_ge(pair("x_in")[j], 16 * (i + 1))
                    dve.bn_stats(st[:, j, :], src[j]).then_inc(sem["ln_step"], 1)
                for j in range(G):
                    stats_in = of(dve, 4 * i + j + 1)
                    dve.wait_ge(sem["consts"], 1)
                    dve.wait_ge(sem["ln_step"], stats_in)
                    dve.bn_aggr(mv[:, j, :], st[:, j, :]).then_inc(sem["ln_step"], 1)
                for j in range(G):
                    dve.wait_ge(sem["ln_step"], 4 * i + 2 + j + 1)
                    ts(vs[:, j, :], mv[:, j, 1:2], EPS, XS ** -2, ALU.add, ALU.mult).then_inc(sem["ln_var"], 1)

            def normal(i, src, ready, done, f):
                base = NORM_STEPS * i
                for j in range(G):
                    dve.wait_ge(ready, 2 * i + j + 1)
                    dve.bn_stats(st[:, j, :], src[:, j, :]).then_inc(done, 1)
                for j in range(G):
                    stats_in = of(dve, base + j + 1)
                    dve.wait_ge(sem["consts"], 1)
                    dve.wait_ge(done, stats_in)
                    dve.bn_aggr(mv[:, j, :], st[:, j, :]).then_inc(done, 1)
                dve.wait_ge(done, base + 4)
                ts(vs[:], mv[:, :, 1:2], EPS, f, ALU.add, ALU.mult).then_inc(done, 1)
                dve.wait_ge(done, base + 5)
                ts(rs[:].bitcast(I32), vs[:].bitcast(I32), -0.5, float(0x5F3759DF), ALU.mult, ALU.add).then_inc(done, 1)
                for n in range(NEWTON):
                    dve.wait_ge(done, base + 6 + 3 * n)
                    stt(y0[:, :, None], rs[:], -0.5, rs[:], ALU.mult, ALU.mult).then_inc(done, 1)
                    dve.wait_ge(done, base + 7 + 3 * n)
                    tt(y0[:, :, None], y0[:, :, None], vs[:], ALU.mult).then_inc(done, 1)
                    dve.wait_ge(done, base + 8 + 3 * n)
                    stt(rs[:], y0[:, :, None], 1.5, rs[:], ALU.add, ALU.mult).then_inc(done, 1)

            def rows_a(i):
                statistics(i, xa)
                for j in range(G):
                    dve.wait_ge(sem["ln_rs"], 2 * i + j + 1)
                    if past(i):
                        dve.wait_ge(sem["xn_hi"], 2 * i + j - 1)
                    if past(i):
                        dve.wait_ge(sem["xt_ps"], 2 * i + j - 1)
                    ts(xn[j], xa[j], mv[:, j, 0:1], rs[:, j, :], ALU.subtract, ALU.mult).then_inc(sem["ln_out"], 1)
                for j in range(G):
                    dve.wait_ge(sem["xn_hi"], 2 * i + j + 1)
                    tt(tab[j][:, D:2 * D], xn[j], tab[j][:, 0:D], ALU.subtract).then_inc(sem["xn_lo"], 1)

            def keys(i):
                for j in range(G):
                    dve.wait_ge(sem["k_ps"], 2 * i + j + 1)
                    ts(ke[j], bank[2 + j][0:T, :], sv[0:T, S_KV:S_KV + 1], 0.0, ALU.mult, ALU.min).then_inc(sem["k_neg"], 1)
                for j in range(G):
                    dve.wait_ge(sem["k_relu"], 2 * i + j + 1)
                    dve.wait_ge(sem["k_exp"], 2 * i + j + 1)
                    dve.wait_ge(sem["ctx_ps"], 2 * i + 1)
                    dve.wait_ge(sem["ksum_add"], 2 * i + 1)
                    tt(kf[j], ke[j], kr[j], ALU.add).then_inc(sem["kf"], 1)

            def counts(i):
                for j in range(G):
                    if past(2 * i + j):
                        dve.wait_ge(sem["edge_cnt"], 2 * i + j)
                    ts(junk[0:EP, :], d_f[0:EP, :], thr[0:EP, bass.ds(2 * i + j + 1, 1)], 0.0, ALU.is_lt, ALU.add,
                       accum_out=cnt[0:EP, bass.ds(2 * i + j + 1, 1)]).then_inc(sem["edge_cnt"], 1)

            def lo_t(i):
                for j in range(G):
                    dve.wait_ge(sem["xt_hi"], 2 * i + j + 1)
                    tt(xT[:, 1, :, both(j)], four(j), xT[:, 0, :, both(j)], ALU.subtract).then_inc(sem["xt_lo"], 1)

            rows_a(0)
            lo_t(0)
            counts(0)
            with dve.Fori(0, NG - 1) as i:
                rows_a(i + 1)
                keys(i)
                lo_t(i + 1)
                counts(i + 1)
            keys(NG - 1)

            dve.wait_ge(sem["edge_sum"], 1)
            CS, ST, EN, KA, KB, U = (row[:, r, :] for r in range(6))
            dve.tensor_copy(CS[:, 0:52], bank[5][0:1, 0:52]).then_inc(sem["edge_step"], 1)
            dve.memset(KA[:], 0.0).then_inc(sem["edge_step"], 1)
            dve.memset(KB[:], 0.0).then_inc(sem["edge_step"], 1)
            dve.wait_ge(sem["edge_step"], 3)
            dve.memset(CS[:, NT:NT + 1], float(E_EDGES)).then_inc(sem["edge_step"], 1)
            ts(U[:, 0:1], CS[:, 51:52], 1.0, None, ALU.min).then_inc(sem["edge_step"], 1)
            dve.wait_ge(sem["edge_step"], 5)
            ts(U[:, 1:2], U[:, 0:1], -1.0, 1.0, ALU.mult, ALU.add).then_inc(sem["edge_step"], 1)
            ts(U[:, 2:3], U[:, 0:1], float(E_EDGES), None, ALU.mult).then_inc(sem["edge_step"], 1)
            dve.wait_ge(sem["edge_step"], 7)
            ts(ST[:, 0:NT], CS[:, 0:NT], U[:, 1:2], None, ALU.mult).then_inc(sem["edge_step"], 1)
            ts(EN[:, 0:NT], CS[:, 1:NT + 1], U[:, 1:2], U[:, 2:3], ALU.mult, ALU.add).then_inc(sem["edge_step"], 1)
            dve.wait_ge(sem["edge_step"], 9)
            tt(EN[:, 0:NT], EN[:, 0:NT], ST[:, 0:NT], ALU.subtract).then_inc(sem["edge_step"], 1)
            dve.wait_ge(sem["edge_step"], 10)
            ts(EN[:, 0:NT], EN[:, 0:NT], SPAN - 1.0, 1.0 / SPAN, ALU.add, ALU.mult).then_inc(sem["edge_step"], 1)
            dve.wait_ge(sem["edge_step"], 11)
            ts(sched[:, 1, 0:NT], EN[:, 0:NT], -0.5 + 1.0 / 8192, 1.0, ALU.add, ALU.max).then_inc(sem["edge_step"], 1)
            dve.wait_ge(sem["edge_step"], 12)
            dve.tensor_copy(KA[:, 1:NT + 1], sched[:, 1, 0:NT]).then_inc(sem["edge_step"], 1)
            a, b, d, n = KA, KB, 1, 13
            while d < NT + 1:
                dve.wait_ge(sem["edge_step"], n)
                dve.tensor_copy(b[:, 0:d], a[:, 0:d]).then_inc(sem["edge_step"], 1)
                tt(b[:, d:NT + 1], a[:, d:NT + 1], a[:, 0:NT + 1 - d], ALU.add).then_inc(sem["edge_step"], 1)
                a, b, d, n = b, a, 2 * d, n + 2
            dve.wait_ge(sem["edge_step"], n)
            dve.tensor_copy(sched[:, 1, 0:NT + 1], a[:, 0:NT + 1]).then_inc(sem["edge_step"], 1)
            dve.wait_ge(sem["edge_step"], n + 1)
            dve.tensor_copy(sched[:, 0, 0:NT], ST[:, 0:NT]).then_inc(sem["sched_set"], 1)


            def onehots(g, j):
                t = 2 * g + j
                lo = dve.value_load(sched[0:1, 1, bass.ds(t, 1)], min_val=0, max_val=4000)
                hi = dve.value_load(sched[0:1, 1, bass.ds(t + 1, 1)], min_val=1, max_val=4000)
                value = of(dve, 3 + t)
                dve.wait_ge(sem["consts"], 1)
                dve.wait_ge(sem["iota_set"], value)
                with dve.Fori(lo, hi) as r:
                    dve.wait_ge(sem["e_in"], (r + 1) * 16)
                    dve.wait_ge(sem["agg_ps"], r + 1)
                    tt(oh, iota_f[:, None, :].broadcast_to([128, SLOTS, T]),
                       ebuf[j][:, 1:2 * SLOTS:2][:, :, None].broadcast_to([128, SLOTS, T]), ALU.is_equal).then_inc(sem["onehot"], 1)
                    dve.wait_ge(sem["onehot"], r + 1)
                    with nc.allow_low_precision("counts of at most 17 are whole numbers in float16"):
                        dve.tensor_reduce(ohc[:], oh.rearrange("p s n -> p n s"), AX_X, ALU.add).then_inc(sem["onehot_cnt"], 1)
                ts(iota_f[:], iota_f[:], float(T), None, ALU.add).then_inc(sem["iota_set"], 1)

            dve.wait_ge(sem["ctx_ps"], 2 * NG + 1)
            tt(ctxT, bank[6][:, :].rearrange("p (k n) -> p k n", k=KC), blk[:, None, :].broadcast_to([128, KC, 128]),
               ALU.mult).then_inc(sem["ctx_sb"], 1)
            dve.wait_ge(sem["wout_in"], 32)
            dve.wait_ge(sem["rows_in"], 48)
            tt(beta_bc[0:T, :], beta_bc[0:T, :], Mf[0:T, 0, :], ALU.add).then_inc(sem["beta_set"], 1)
            dve.wait_ge(sem["ksum_ps"], 1)
            ts(ksum[:], bank[7][:, 0:KC], 1e-30, None, ALU.max).then_inc(sem["ksum_sb"], 1)
            dve.wait_ge(sem["ksum_sb"], 1)
            dve.reciprocal(kinv[:], ksum[:]).then_inc(sem["kinv_set"], 1)
            dve.wait_ge(sem["kinv_set"], 1)
            dve.wait_ge(sem["beta_set"], 1)
            for p in range(KC):
                dve.wait_ge(sem["m_ps"], p + 1)
                ts(Mf[:, p, :], bank[p][:, :], kinv[:, p:p + 1], None, ALU.mult).then_inc(sem["mf_set"], 1)
            dve.wait_ge(sem["mf_set"], KC)
            dve.tensor_reduce(mg[:, MH:MH + 1], Mf.rearrange("p k n -> p (k n)"), AX_X, ALU.max,
                              apply_absolute_value=True).then_inc(sem["mf_max"], 1)
            dve.wait_ge(sem["disp_set"], 4)
            dve.wait_ge(sem["slots_out"], 32)
            dve.wait_ge(sem["sched_set"], 1)
            onehots(0, 0)
            dve.wait_ge(sem["mh_all"], 1)
            scales(MH, MH + 1, sem["mh_scale"], 0)
            ts(sv[:, S_ATT:S_ATT + 1], si[:, MH:MH + 1], 1 / QS, None, ALU.mult).then_inc(sem["mh_scale"], 1)
            dve.wait_ge(sem["mh_hi"], 1)
            stt(Mh[:, 1].rearrange("p k n -> p (k n)"), Mf.rearrange("p k n -> p (k n)"), sg[:, MH:MH + 1],
                Mh[:, 0].rearrange("p k n -> p (k n)"), ALU.mult, ALU.subtract).then_inc(sem["mh_done"], 1)
            dve.wait_ge(sem["mh_done"], 1)

            def means(g, j):
                dve.wait_ge(sem["agg_end"], 2 * g + j + 1)
                ts(dg[:, j, 0:1], bank[7][0:T, 0:1], 1.0, None, ALU.max).then_inc(sem["deg_step"], 1)
                dve.wait_ge(sem["deg_step"], 4 * g + 2 * j + 1)
                dve.reciprocal(dg[:, j, 1:2], dg[:, j, 0:1]).then_inc(sem["deg_step"], 1)
                dve.wait_ge(sem["deg_step"], 4 * g + 2 * j + 2)
                if past(g):
                    dve.wait_ge(sem["mt_ps"], 2 * g)
                ts(mean[:, j, :], bank[6][0:T, :], dg[:, j, 1:2], None, ALU.mult).then_inc(sem["mean_sb"], 1)

            def split_normalised(i):
                for j in range(G):
                    dve.wait_ge(sem["tn_hi"], 2 * i + j + 1)
                    tt(tab2[:, j, D:2 * D], tn[:, j, :], tab2[:, j, 0:D], ALU.subtract).then_inc(sem["tn_lo"], 1)

            def gate(i):
                done, base = sem["gate_dve"], GATE_STEPS * i
                dve.wait_ge(sem["gate_ps"], 2 * i + 2)
                stt(gl[:], bank[2][0:T, 0:16].rearrange("p (j e) -> p j e", j=G), sv[0:T, S_G:S_G + 1],
                    gateb_bc[0:T, None, :].broadcast_to([T, G, NE]), ALU.mult, ALU.add).then_inc(done, 1)
                logits_in = of(dve, base + 1)
                dve.wait_ge(sem["consts"], 1)
                dve.wait_ge(done, logits_in)
                for j in range(G):
                    dve.max(g8[:, j, :], gl[:, j, :]).then_inc(done, 1)
                largest_in = of(dve, base + 3)
                dve.wait_ge(sem["consts"], 1)
                dve.wait_ge(done, largest_in)
                for j in range(G):
                    dve.max_index(gi[:, j, :], g8[:, j, :], gl[:, j, :]).then_inc(done, 1)
                ts(gs[:, :, 0:1], g8[:, :, 0:1], -1.0, None, ALU.mult).then_inc(done, 1)
                dve.wait_ge(done, base + 5)
                dve.tensor_copy(gif[:], gi[:, :, 0:2]).then_inc(done, 1)
                dve.wait_ge(done, base + 7)
                tt(choice[:], iota_e[0:T, None, None, :].broadcast_to([T, G, 2, NE]),
                   gif[:, :, :, None].broadcast_to([T, G, 2, NE]), ALU.is_equal).then_inc(done, 1)
                dve.wait_ge(done, base + 8)
                tt(chosen[:], choice[:, :, 0, :], choice[:, :, 1, :], ALU.add).then_inc(done, 1)
                dve.wait_ge(sem["gate_exp"], 4 * i + 4)
                dve.reciprocal(gs[:, :, 2:3], gs[:, :, 1:2]).then_inc(done, 1)
                dve.wait_ge(done, base + 10)
                tt(wk[:, bass.ds(2 * i, 2), :], ew[:], gs[:, :, 2:3].broadcast_to([T, G, 2]), ALU.mult).then_inc(done, 1)

            def places(i):
                done, base = sem["gate_dve"], GATE_STEPS * i
                dve.wait_ge(sem["pos_ps"], i + 1)
                tt(place[:], bank[3][0:T, 0:16].rearrange("p (j e) -> p j e", j=G),
                   eoff[0:T, None, :].broadcast_to([T, G, NE]), ALU.add).then_inc(done, 1)
                dve.wait_ge(done, base + 12)
                tt(placed[:], choice[:], place[:, :, None, :].broadcast_to([T, G, 2, NE]), ALU.mult).then_inc(done, 1)
                dve.wait_ge(done, base + 13)
                dve.tensor_reduce(posf[:], placed[:], AX_X, ALU.add).then_inc(done, 1)
                dve.wait_ge(done, base + 14)
                if past(i):
                    dve.wait_ge(sem["scat"], 64 * i)
                dve.tensor_copy(posi[:], posf[:]).then_inc(done, 1)
                dve.tensor_copy(pos[:, bass.ds(2 * i, 2), :], posf[:]).then_inc(done, 1)
                ts(tok[:], tok[:], GT, None, ALU.add).then_inc(done, 1)
                tt(before[:], before[:], chosen[:, 0, :], ALU.add).then_inc(done, 1)
                dve.wait_ge(done, base + 18)
                tt(before[:], before[:], chosen[:, 1, :], ALU.add).then_inc(done, 1)
                assert GATE_STEPS == 19

            def group(i, prev, nxt):
                for c in range(2):
                    cc = slice(2 * c, 2 * c + 2)
                    dve.wait_ge(sem["q_ps"], 2 * i + c + 1)
                    if past(i):
                        dve.wait_ge(sem["q_lo"], 2 * i)
                        dve.wait_ge(sem["q_hi"], 2 * i)
                    ts(qe[:, cc, :], two(4 + c), sv[:, S_Q:S_Q + 1], 0.0, ALU.mult, ALU.min).then_inc(sem["q_neg"], 1)
                for j in range(G):
                    dve.wait_ge(sem["mt_hi"], 2 * i + j + 1)
                    tt(mT[:, 1, :, both(j)], four(2 + j), mT[:, 0, :, both(j)], ALU.subtract).then_inc(sem["mt_lo"], 1)
                for c in range(2):
                    cc = slice(2 * c, 2 * c + 2)
                    dve.wait_ge(sem["q_exp"], 2 * i + c + 1)
                    dve.wait_ge(sem["q_relu"], 2 * i + c + 1)
                    tt(qe[:, cc, :], qe[:, cc, :], qr[:, cc, :], ALU.add).then_inc(sem["q_phi"], 1)
                if prev is not None:
                    split_normalised(prev)
                if nxt is not None:
                    onehots(nxt, 0)
                for c in range(2):
                    cc = slice(2 * c, 2 * c + 2)
                    dve.wait_ge(sem["q_den"], 2 * i + c + 1)
                    dve.reciprocal(qr[:, cc, :], qr[:, cc, :]).then_inc(sem["q_rec"], 1)
                    dve.wait_ge(sem["q_rec"], 2 * i + c + 1)
                    stt(qe[:, cc, :], qe[:, cc, :], QS, qr[:, cc, :], ALU.mult, ALU.mult).then_inc(sem["q_hat"], 1)
                for c in range(2):
                    cc = slice(2 * c, 2 * c + 2)
                    dve.wait_ge(sem["q_hi"], 2 * i + c + 1)
                    tt(qh[:, 1, cc, :], qe[:, cc, :], qh[:, 0, cc, :], ALU.subtract).then_inc(sem["q_lo"], 1)
                if nxt is not None:
                    means(nxt, 0)
                if prev is not None:
                    gate(prev)
                if nxt is not None:
                    onehots(nxt, 1)
                for j in range(G):
                    dve.wait_ge(sem["h_ps"], 2 * i + j + 1)
                    stt(hh[:, j, :], bank[4 + j][0:T, :], sv[0:T, S_H:S_H + 1], bias_bc[0:T, :], ALU.mult, ALU.add).then_inc(sem["h_sb"], 1)
                normal(i, hh, sem["h_sb"], sem["h_step"], 1.0)
                for j in range(G):
                    stt(hh[:, j, :], hh[:, j, :], mv[:, j, 0:1], gamma_bc[0:T, :], ALU.subtract, ALU.mult).then_inc(sem["h_gam"], 1)
                dve.wait_ge(sem["h_step"], NORM_STEPS * (i + 1))
                dve.wait_ge(sem["xb"], i + 1)
                for j in range(G):
                    dve.wait_ge(sem["h_gam"], 2 * i + j + 1)
                    stt(hh[:, j, :], hh[:, j, :], rs[:, j, :], xg[:, j, :], ALU.mult, ALU.add).then_inc(sem["h_res"], 1)
                for j in range(G):
                    dve.wait_ge(sem["h_res"], 2 * i + j + 1)
                    dve.wait_ge(sem["att_ps"], 2 * i + j + 1)
                    if past(i):
                        dve.wait_ge(sem["x2_out"], 16 * i)
                    stt(x2[:, j, :], bank[j][0:T, :], sv[0:T, S_ATT:S_ATT + 1], hh[:, j, :], ALU.mult, ALU.add).then_inc(sem["x2_sb"], 1)
                normal(i, x2, sem["x2_sb"], sem["z_step"], XS ** -2)
                dve.wait_ge(sem["z_step"], NORM_STEPS * (i + 1))
                for j in range(G):
                    if past(i):
                        dve.wait_ge(sem["tn_lo"], 2 * i)
                    ts(tn[:, j, :], x2[:, j, :], mv[:, j, 0:1], rs[:, j, :], ALU.subtract, ALU.mult).then_inc(sem["tn_sb"], 1)
                if nxt is not None:
                    means(nxt, 1)
                if prev is not None:
                    places(prev)

            means(0, 0)
            onehots(0, 1)
            means(0, 1)
            group(0, None, 1)
            group(1, 0, 2)
            with dve.Fori(2, NG - 1) as i:
                group(i, i - 1, i + 1)
            group(NG - 1, NG - 2, None)
            split_normalised(NG - 1)
            gate(NG - 1)
            places(NG - 1)

            CN, KA, KB, SH = (row2[:, r, :] for r in range(4))
            P0, P1, P2 = (after[:, r, :] for r in range(3))
            stepped = sem["cnt_step"]
            dve.wait_ge(sem["agg_end"], NT)
            dve.wait_ge(sem["cnt_ps"], 1)
            ts(CN[:, 0:NE], bank[2][0:T, 0:NE], CH - 1.0, 1.0 / CH, ALU.add, ALU.mult).then_inc(stepped, 1)
            dve.memset(KA, 0.0).then_inc(stepped, 1)
            dve.memset(KB, 0.0).then_inc(stepped, 1)
            dve.wait_ge(stepped, 3)
            ts(sched2[:, 0:NE], CN[:, 0:NE], -0.5 + 0.5 / CH, 2.0, ALU.add, ALU.max).then_inc(stepped, 1)
            dve.wait_ge(sem["gate_dve"], GATE_STEPS * NG)
            dve.tensor_copy(P0, pos[:].rearrange("p t k -> p (t k)")).then_inc(stepped, 1)
            dve.wait_ge(stepped, 5)
            dve.tensor_copy(KA[:, 1:NE + 1], sched2[:, 0:NE]).then_inc(stepped, 1)
            ts(SH[:, 0:NE], sched2[:, 0:NE], float(CH), -float(CAP), ALU.mult, ALU.add).then_inc(stepped, 1)
            dve.tensor_copy(P2, P0).then_inc(stepped, 1)
            n = 8
            for e in range(1, NE):
                dve.wait_ge(stepped, n)
                ts(P1, P0, float(e * CAP), SH[:, e - 1:e], ALU.is_ge, ALU.mult).then_inc(stepped, 1)
                dve.wait_ge(stepped, n + 1)
                tt(P2, P2, P1, ALU.add).then_inc(stepped, 1)
                n += 2
            a, b, d = KA, KB, 1
            while d < NE + 1:
                dve.wait_ge(stepped, n)
                dve.tensor_copy(b[:, 0:d], a[:, 0:d]).then_inc(stepped, 1)
                tt(b[:, d:NE + 1], a[:, d:NE + 1], a[:, 0:NE + 1 - d], ALU.add).then_inc(stepped, 1)
                a, b, d, n = b, a, 2 * d, n + 2
            dve.wait_ge(stepped, n)
            dve.tensor_copy(pos[:].rearrange("p t k -> p (t k)"), P2).then_inc(sem["yd_pos"], 1)
            dve.tensor_copy(sched2[:, 0:NE + 1], a[:, 0:NE + 1]).then_inc(sem["sched2_set"], 1)

            dve.wait_ge(sem["agg_end"], NT)
            dve.wait_ge(sem["b2_in"], 16 * NE)
            dve.wait_ge(sem["sched2_set"], 1)

            def turned_rows(r):
                dve.wait_ge(sem["ct_ps"], 2 * r + 2)
                if past(r):
                    dve.wait_ge(sem["ch_ps"], r)
                dve.tensor_copy(tTc[:, :, :, 128:256], parts16(3, 128)).then_inc(sem["ct_dve"], 1)

            def made(e, n):
                for j in range(2):
                    dve.wait_ge(sem["cp_ps"], 2 * n + j)
                    dve.wait_ge(sem["y_st"], n * 16)
                    stt(ysb[:, j, :], bank[4 + j][:, :], sv[:, S_W2:S_W2 + 1], b2bc[:, e, :], ALU.mult, ALU.add).then_inc(sem["y_sb"], 1)

            def low(r):
                dve.wait_ge(sem["c_hi"], r + 1)
                stt(hTc[:, 1], gelc, sg[:, HB:HB + 1], hTc[:, 0], ALU.mult, ALU.subtract).then_inc(sem["c_lo"], 1)

            turned_rows(0)
            for e in range(NE):
                lo = dve.value_load(sched2[0:1, e:e + 1], min_val=2 * e, max_val=400) if e else 0
                hi = dve.value_load(sched2[0:1, e + 1:e + 2], min_val=2 * e + 2, max_val=400)
                turned_rows(lo + 1)
                if e:
                    made(e - 1, lo)
                low(lo)
                with dve.Fori(lo + 1, hi) as r:
                    turned_rows(r + 1)
                    made(e, r)
                    low(r)
            made(NE - 1, hi)

            dve.wait_ge(sem["sb2_in"], 32)
            tt(sb2[:, 0, :], sb2[:, 0, :], sb2[:, 1, :], ALU.add).then_inc(sem["sb2_sum"], 1)
            dve.wait_ge(sem["sb2_sum"], 1)

            def combine(i):
                for e in range(NS):
                    dve.wait_ge(sem["d_hi"], 2 * i + e + 1)
                    stt(hTd[e][:, 1], geld[e], sg[:, HB:HB + 1], hTd[e][:, 0], ALU.mult, ALU.subtract).then_inc(sem["d_lo"], 1)
                dve.wait_ge(sem["dx_in"], 16 * (i + 1))
                tt(acc, acc, sb2[:, 0:1, :].broadcast_to([T, G, D]), ALU.add).then_inc(sem["sb2_sum"], 1)
                dve.wait_ge(sem["yg_in"], 64 * (i + 1))
                dve.wait_ge(sem["sb2_sum"], i + 2)
                for k in range(2):
                    for j in range(G):
                        if k:
                            dve.wait_ge(sem["d_y"], 4 * i + j + 1)
                        stt(acc[:, j, :], yr[:, j, k, :], wcur[:, 2 * j + k:2 * j + k + 1], acc[:, j, :], ALU.mult, ALU.add).then_inc(sem["d_y"], 1)
                for j in range(G):
                    dve.wait_ge(sem["d_y"], 4 * i + 3 + j)
                    dve.wait_ge(sem["d_f2"], 2 * i + j + 1)
                    if past(i):
                        dve.wait_ge(sem["d_out"], 16 * i)
                    stt(res[:, j, :], bank[2 + j][0:T, :], sv[0:T, S_W2:S_W2 + 1], acc[:, j, :], ALU.mult, ALU.add).then_inc(sem["d_res"], 1)

            combine(0)
            with dve.Fori(1, NG) as i:
                combine(i)


GATE_STEPS = 19
NORM_STEPS = 6 + 3 * NEWTON


def kernel(**inputs):
    import numpy as np
    import concourse.bacc as bacc
    from concourse.bass_utils import run_bass_kernel_spmd

    a = {k: np.asarray(v) for k, v in inputs.items()}

    def by_rows(w):
        r, n = w.shape
        return np.ascontiguousarray(w.reshape(r // 128, 128, n).transpose(1, 0, 2).reshape(128, -1))

    src = np.concatenate([a["src"], np.zeros(SPAN, np.int32)]).astype(np.int32)
    dst = np.concatenate([a["dst"], np.full(SPAN, N, np.int32)]).astype(np.int32)
    w1 = np.concatenate([a["L0_ffn_sw1"], a["L0_ffn_rw1"]]).reshape(HID, D)
    w2 = np.concatenate([a["L0_ffn_sw2"], a["L0_ffn_rw2"]]).transpose(0, 2, 1).reshape(HID, D)
    b1 = np.concatenate([a["L0_ffn_sb1"], a["L0_ffn_rb1"]]).reshape(FC, 128)
    qkv = a["L0_mix_w_qkv"]
    arrays = {
        "x": a["x"],
        "edges": np.stack([src, dst], 1).reshape(-1),
        "dst_flat": dst,
        "w_kv": by_rows(qkv[D:].T),
        "w_q": by_rows(qkv[:D].T),
        "w_sn": np.concatenate([by_rows(a["L0_gnn_W_self"].T), by_rows(a["L0_gnn_W_neigh"].T)], 1),
        "w_out": by_rows(a["L0_mix_w_out"].T),
        "w_gate": by_rows(a["L0_ffn_gate_w"].T),
        "w_1": by_rows(w1.T),
        "w_2": by_rows(w2),
        "b_1": np.ascontiguousarray(b1.T),
        "b_2": np.concatenate([a["L0_ffn_rb2"], a["L0_ffn_sb2"]]),
        "rows": np.stack([a["L0_gnn_bias"], a["L0_gnn_gamma"], a["L0_gnn_beta"], a["L0_mix_b_out"]]),
        "gate_b": a["L0_ffn_gate_b"].reshape(1, NE),
    }
    arrays = {k: np.ascontiguousarray(v) for k, v in arrays.items()}
    nc = bacc.Bacc("TRN2", target_bir_lowering=False, num_devices=1)
    args = [nc.dram_tensor(k, v.shape, mybir.dt.from_np(v.dtype), kind="ExternalInput").ap() for k, v in arrays.items()]
    args.append(nc.dram_tensor("out", [N, D], F32, kind="ExternalOutput").ap())
    gps_layer_kernel(nc, *args)
    r = run_bass_kernel_spmd(nc, [arrays], core_ids=[0])
    return r.results[0]["out"]
```
